# Optimizing a Trainium2 kernel written in Bass

```python
import numpy as np
import jax
import jax.numpy as jnp

def _softmax(x, axis=-1):
    return jax.nn.softmax(x, axis=axis)

def _gelu(x):
    return jax.nn.gelu(x, approximate=True)

def _silu(x):
    return jax.nn.silu(x)

def _sigmoid(x):
    return jax.nn.sigmoid(x)

def _layernorm(x, axis=-1, eps=1e-05):
    m = jnp.mean(x, axis=axis, keepdims=True)
    v = jnp.var(x, axis=axis, keepdims=True)
    return (x - m) / jnp.sqrt(v + eps)

def _scatter_add(tgt, idx, src, axis=0):
    return tgt.at[idx].add(src)

def _segment_sum(src, seg, n):
    return jax.ops.segment_sum(src, seg, n)
kernel_name = 'mk_flamingo_gated_d1_seqx_r2_27f913'

def setup_inputs(seed: int=0):
    np.random.seed(seed)
    _w = jnp.asarray

    def _rec_inputs():
        import jax
        import jax.numpy as jnp
        _rk = jax.random.key(seed)
        x = -0.0005207 + 1.001 * jax.random.normal(jax.random.fold_in(_rk, 1), (8, 512, 512), jnp.float32)
        _lenS = 512 - jax.random.randint(jax.random.fold_in(_rk, 7), (8,), 0, max(1, 512 // 4) + 1, jnp.int32)
        _lenS2 = 512 - jax.random.randint(jax.random.fold_in(_rk, 8), (8,), 0, max(1, 512 // 4) + 1, jnp.int32)
        _ctx_1024P = jax.random.normal(jax.random.fold_in(_rk, 11), (8, 16, 512), jnp.float32)
        _ctx_1024c = jax.random.dirichlet(jax.random.fold_in(_rk, 511), 0.3 * jnp.ones((16,), jnp.float32), (8, 512))
        _ctx_1024t = jnp.einsum('bsk,bkd->bsd', _ctx_1024c, _ctx_1024P)
        _ctx_1024t = _ctx_1024t * jax.lax.rsqrt(jnp.mean(jnp.square(_ctx_1024t)) + 1e-12) * 0.953939
        ctx_1024 = -1.39393e-06 + 0.999914 * (_ctx_1024t + 0.3 * jax.random.normal(jax.random.fold_in(_rk, 611), (8, 512, 512), jnp.float32))
        _g = jax.random.normal(jax.random.fold_in(_rk, 9001), (2, 1), jnp.float32)
        _g = jnp.sign(_g) * jnp.maximum(jnp.abs(_g), 1.0) + (_g == 0) * 1.0
        g_xattn = _g[0]
        g_ffn = _g[1]
        return (x, ctx_1024, g_xattn, g_ffn)
    x, ctx_1024, g_xattn, g_ffn = _rec_inputs()

    def _L0_xattn_setup():
        import jax, jax.numpy as jnp
        import numpy as np
        DIM = 512
        HEADS = 16
        HEAD_DIM = DIM // HEADS
        SCALE = HEAD_DIM ** (-0.5)
        key = jax.random.key(seed)
        ks = jax.random.split(key, 6)
        B, Nq, Nkv = (2, 512, 1024)
        s = DIM ** (-0.5)
        return {'x': jax.random.normal(ks[0], (B, Nq, DIM), jnp.float32), 'mem': jax.random.normal(ks[1], (B, Nkv, DIM), jnp.float32), 'W_kv': jax.random.normal(ks[2], (DIM, 2 * DIM), jnp.float32) * s, 'W_q': jax.random.normal(ks[3], (DIM, DIM), jnp.float32) * s, 'W_proj': jax.random.normal(ks[4], (DIM, DIM), jnp.float32) * s, 'b_proj': jax.random.normal(ks[5], (DIM,), jnp.float32) * 0.01}
    _L0_xattn_all = _L0_xattn_setup()
    _L0_xattn_in = {k: v for k, v in _L0_xattn_all.items() if k in ('W_kv', 'W_q', 'W_proj', 'b_proj')}
    del _L0_xattn_all

    def _L0_ffn_setup():
        import jax, jax.numpy as jnp
        import numpy as np
        B, T, C = (2, 1024, 512)
        H, D = (16, 64)
        CR = 8
        R = C // CR
        ROPE = D // 2
        NOPE = D - ROPE
        E, K, I, S = (8, 2, 256, 1)
        THETA = 100000.0
        EPS = 1e-05

        def _rmsnorm(x, w):
            rms = jnp.sqrt(jnp.mean(x * x, axis=-1, keepdims=True) + EPS)
            return w * (x / rms)

        def _rope(xh):
            d = xh.shape[-1]
            t = jnp.arange(xh.shape[2], dtype=jnp.float32)
            freqs = 1.0 / THETA ** (jnp.arange(0, d, 2, dtype=jnp.float32) / d)
            ang = jnp.outer(t, freqs)
            cos, sin = (jnp.cos(ang), jnp.sin(ang))
            xr = xh.reshape(xh.shape[:-1] + (d // 2, 2))
            x0, x1 = (xr[..., 0], xr[..., 1])
            rot = jnp.stack([x0 * cos - x1 * sin, x0 * sin + x1 * cos], axis=-1)
            return rot.reshape(xh.shape)

        def _attention(x, Wq, Wkva, Wkvb, Wo):
            b, t, _ = x.shape
            q = (x @ Wq).reshape(b, t, H, D).transpose(0, 2, 1, 3)
            ckv = x @ Wkva
            kv_latent, k_rope = (ckv[:, :, :R], ckv[:, :, R:])
            kv = (kv_latent @ Wkvb).reshape(b, t, H, NOPE).transpose(0, 2, 1, 3)
            k_rope = jnp.broadcast_to(k_rope[:, None, :, :], (b, H, t, ROPE))
            q_nope, q_rope = (q[..., :NOPE], q[..., NOPE:])
            q = jnp.concatenate([q_nope, _rope(q_rope)], axis=-1)
            k = jnp.concatenate([kv, _rope(k_rope)], axis=-1)
            v = jnp.concatenate([kv, jnp.zeros_like(k_rope)], axis=-1)
            att = jnp.einsum('bhqd,bhkd->bhqk', q, k) / jnp.sqrt(jnp.float32(D))
            mask = jnp.tril(jnp.ones((t, t), dtype=bool))
            att = jnp.where(mask, att, jnp.float32(-jnp.inf))
            att = jax.nn.softmax(att, axis=-1)
            y = jnp.einsum('bhqk,bhkd->bhqd', att, v)
            y = y.transpose(0, 2, 1, 3).reshape(b, t, H * D)
            return y @ Wo

        def _experts(x_flat, Wg, Wu, Wd):
            g = jax.nn.silu(jnp.einsum('nc,eci->nei', x_flat, Wg))
            u = jnp.einsum('nc,eci->nei', x_flat, Wu)
            return jnp.einsum('nei,eic->nec', g * u, Wd)

        def _moe(x, Wgate, expert_bias, Wg, Wu, Wd, sWg, sWu, sWd):
            b, t, c = x.shape
            xf = x.reshape(-1, c)
            shared = jnp.mean(_experts(xf, sWg, sWu, sWd), axis=1)
            logits = xf @ Wgate + expert_bias
            probs = jax.nn.softmax(logits, axis=-1)
            topk_p, topk_i = jax.lax.top_k(probs, K)
            topk_p = topk_p / jnp.sum(topk_p, axis=-1, keepdims=True)
            comb = jnp.sum(jax.nn.one_hot(topk_i, E, dtype=xf.dtype) * topk_p[..., None], axis=1)
            routed = jnp.einsum('ne,nec->nc', comb, _experts(xf, Wg, Wu, Wd))
            return (shared + routed).reshape(b, t, c)
        key = jax.random.key(seed)
        ks = jax.random.split(key, 16)
        w = lambda k, shp: jax.random.normal(k, shp, dtype=jnp.float32) * 0.02
        return {'x': jax.random.normal(ks[0], (B, T, C), dtype=jnp.float32), 'w_ln1': jnp.ones((C,), jnp.float32), 'Wq': w(ks[1], (C, H * D)), 'Wkva': w(ks[2], (C, R + ROPE)), 'Wkvb': w(ks[3], (R, H * NOPE)), 'Wo': w(ks[4], (H * D, C)), 'w_ln2': jnp.ones((C,), jnp.float32), 'Wgate': w(ks[5], (C, E)), 'expert_bias': jnp.zeros((E,), jnp.float32), 'Wg': w(ks[6], (E, C, I)), 'Wu': w(ks[7], (E, C, I)), 'Wd': w(ks[8], (E, I, C)), 'sWg': w(ks[9], (S, C, I)), 'sWu': w(ks[10], (S, C, I)), 'sWd': w(ks[11], (S, I, C))}
    _L0_ffn_all = _L0_ffn_setup()
    _L0_ffn_in = {k: v for k, v in _L0_ffn_all.items() if k in ('w_ln1', 'Wq', 'Wkva', 'Wkvb', 'Wo', 'w_ln2', 'Wgate', 'expert_bias', 'Wg', 'Wu', 'Wd', 'sWg', 'sWu', 'sWd')}
    del _L0_ffn_all
    return {'x': x, 'ctx_1024': ctx_1024, 'g_xattn': g_xattn, 'g_ffn': g_ffn, 'L0_xattn_W_kv': _L0_xattn_in['W_kv'], 'L0_xattn_W_q': _L0_xattn_in['W_q'], 'L0_xattn_W_proj': _L0_xattn_in['W_proj'], 'L0_xattn_b_proj': _L0_xattn_in['b_proj'], 'L0_ffn_w_ln1': _L0_ffn_in['w_ln1'], 'L0_ffn_Wq': _L0_ffn_in['Wq'], 'L0_ffn_Wkva': _L0_ffn_in['Wkva'], 'L0_ffn_Wkvb': _L0_ffn_in['Wkvb'], 'L0_ffn_Wo': _L0_ffn_in['Wo'], 'L0_ffn_w_ln2': _L0_ffn_in['w_ln2'], 'L0_ffn_Wgate': _L0_ffn_in['Wgate'], 'L0_ffn_expert_bias': _L0_ffn_in['expert_bias'], 'L0_ffn_Wg': _L0_ffn_in['Wg'], 'L0_ffn_Wu': _L0_ffn_in['Wu'], 'L0_ffn_Wd': _L0_ffn_in['Wd'], 'L0_ffn_sWg': _L0_ffn_in['sWg'], 'L0_ffn_sWu': _L0_ffn_in['sWu'], 'L0_ffn_sWd': _L0_ffn_in['sWd']}

def reference(x, ctx_1024, g_xattn, g_ffn, L0_xattn_W_kv, L0_xattn_W_q, L0_xattn_W_proj, L0_xattn_b_proj, L0_ffn_w_ln1, L0_ffn_Wq, L0_ffn_Wkva, L0_ffn_Wkvb, L0_ffn_Wo, L0_ffn_w_ln2, L0_ffn_Wgate, L0_ffn_expert_bias, L0_ffn_Wg, L0_ffn_Wu, L0_ffn_Wd, L0_ffn_sWg, L0_ffn_sWu, L0_ffn_sWd):
    import jax
    import jax.numpy as jnp

    def _L0_xattn_ref(x, mem, W_kv, W_q, W_proj, b_proj):
        import jax, jax.numpy as jnp
        import numpy as np
        DIM = 512
        HEADS = 16
        HEAD_DIM = DIM // HEADS
        SCALE = HEAD_DIM ** (-0.5)
        B, Nkv, C = mem.shape
        Nq = x.shape[1]
        kv = (mem @ W_kv).reshape(B, Nkv, 2, HEADS, HEAD_DIM)
        k = kv[:, :, 0].transpose(0, 2, 1, 3)
        v = kv[:, :, 1].transpose(0, 2, 1, 3)
        q = (x @ W_q).reshape(B, Nq, HEADS, HEAD_DIM).transpose(0, 2, 1, 3)
        attn = jnp.einsum('bhqd,bhkd->bhqk', q, k) * SCALE
        attn = jax.nn.softmax(attn, axis=-1)
        out = jnp.einsum('bhqk,bhkd->bhqd', attn, v)
        out = out.transpose(0, 2, 1, 3).reshape(B, Nq, C)
        return out @ W_proj + b_proj

    def _L0_ffn_ref(x, w_ln1, Wq, Wkva, Wkvb, Wo, w_ln2, Wgate, expert_bias, Wg, Wu, Wd, sWg, sWu, sWd):
        import jax, jax.numpy as jnp
        import numpy as np
        B, T, C = (2, 1024, 512)
        H, D = (16, 64)
        CR = 8
        R = C // CR
        ROPE = D // 2
        NOPE = D - ROPE
        E, K, I, S = (8, 2, 256, 1)
        THETA = 100000.0
        EPS = 1e-05

        def _rmsnorm(x, w):
            rms = jnp.sqrt(jnp.mean(x * x, axis=-1, keepdims=True) + EPS)
            return w * (x / rms)

        def _rope(xh):
            d = xh.shape[-1]
            t = jnp.arange(xh.shape[2], dtype=jnp.float32)
            freqs = 1.0 / THETA ** (jnp.arange(0, d, 2, dtype=jnp.float32) / d)
            ang = jnp.outer(t, freqs)
            cos, sin = (jnp.cos(ang), jnp.sin(ang))
            xr = xh.reshape(xh.shape[:-1] + (d // 2, 2))
            x0, x1 = (xr[..., 0], xr[..., 1])
            rot = jnp.stack([x0 * cos - x1 * sin, x0 * sin + x1 * cos], axis=-1)
            return rot.reshape(xh.shape)

        def _attention(x, Wq, Wkva, Wkvb, Wo):
            b, t, _ = x.shape
            q = (x @ Wq).reshape(b, t, H, D).transpose(0, 2, 1, 3)
            ckv = x @ Wkva
            kv_latent, k_rope = (ckv[:, :, :R], ckv[:, :, R:])
            kv = (kv_latent @ Wkvb).reshape(b, t, H, NOPE).transpose(0, 2, 1, 3)
            k_rope = jnp.broadcast_to(k_rope[:, None, :, :], (b, H, t, ROPE))
            q_nope, q_rope = (q[..., :NOPE], q[..., NOPE:])
            q = jnp.concatenate([q_nope, _rope(q_rope)], axis=-1)
            k = jnp.concatenate([kv, _rope(k_rope)], axis=-1)
            v = jnp.concatenate([kv, jnp.zeros_like(k_rope)], axis=-1)
            att = jnp.einsum('bhqd,bhkd->bhqk', q, k) / jnp.sqrt(jnp.float32(D))
            mask = jnp.tril(jnp.ones((t, t), dtype=bool))
            att = jnp.where(mask, att, jnp.float32(-jnp.inf))
            att = jax.nn.softmax(att, axis=-1)
            y = jnp.einsum('bhqk,bhkd->bhqd', att, v)
            y = y.transpose(0, 2, 1, 3).reshape(b, t, H * D)
            return y @ Wo

        def _experts(x_flat, Wg, Wu, Wd):
            g = jax.nn.silu(jnp.einsum('nc,eci->nei', x_flat, Wg))
            u = jnp.einsum('nc,eci->nei', x_flat, Wu)
            return jnp.einsum('nei,eic->nec', g * u, Wd)

        def _moe(x, Wgate, expert_bias, Wg, Wu, Wd, sWg, sWu, sWd):
            b, t, c = x.shape
            xf = x.reshape(-1, c)
            shared = jnp.mean(_experts(xf, sWg, sWu, sWd), axis=1)
            logits = xf @ Wgate + expert_bias
            probs = jax.nn.softmax(logits, axis=-1)
            topk_p, topk_i = jax.lax.top_k(probs, K)
            topk_p = topk_p / jnp.sum(topk_p, axis=-1, keepdims=True)
            comb = jnp.sum(jax.nn.one_hot(topk_i, E, dtype=xf.dtype) * topk_p[..., None], axis=1)
            routed = jnp.einsum('ne,nec->nc', comb, _experts(xf, Wg, Wu, Wd))
            return (shared + routed).reshape(b, t, c)
        x = x + _attention(_rmsnorm(x, w_ln1), Wq, Wkva, Wkvb, Wo)
        residual = x
        xn = _rmsnorm(x, w_ln2)
        x_out = _moe(xn, Wgate, expert_bias, Wg, Wu, Wd, sWg, sWu, sWd)
        return residual + x_out
    x = x + jnp.tanh(g_xattn[0]) * _L0_xattn_ref(_layernorm(x, axis=-1), ctx_1024, L0_xattn_W_kv, L0_xattn_W_q, L0_xattn_W_proj, L0_xattn_b_proj)
    x = x + jnp.tanh(g_ffn[0]) * _L0_ffn_ref(_layernorm(x, axis=-1), L0_ffn_w_ln1, L0_ffn_Wq, L0_ffn_Wkva, L0_ffn_Wkvb, L0_ffn_Wo, L0_ffn_w_ln2, L0_ffn_Wgate, L0_ffn_expert_bias, L0_ffn_Wg, L0_ffn_Wu, L0_ffn_Wd, L0_ffn_sWg, L0_ffn_sWu, L0_ffn_sWd)
    return x

_drawn_inputs = setup_inputs


def setup_inputs(seed=0):
    import zlib

    import numpy as np

    out = dict(_drawn_inputs(seed))
    spreads = {'L0_ffn_w_ln1': (1.0, 0.6), 'L0_ffn_w_ln2': (1.0, 0.2), 'L0_ffn_expert_bias': (0.0, 0.1)}
    factors = {'L0_xattn_b_proj': 4.928, 'L0_ffn_Wq': 8.0}
    for name, (base, spread) in spreads.items():
        noise = np.random.default_rng([zlib.crc32(name.encode()), seed]).standard_normal(out[name].shape)
        drawn = base * np.exp(spread * noise) if base else spread * noise
        out[name] = jnp.asarray(drawn.astype(out[name].dtype))
    for name, factor in factors.items():
        out[name] = (out[name] * factor).astype(out[name].dtype)
    return out
```

```python
import math
from contextlib import ExitStack

import concourse.bass as bass
from concourse import mybir

ALU = mybir.AluOpType
ACT = mybir.ActivationFunctionType
AX_X = mybir.AxisListType.X
F32 = mybir.dt.float32
F32R = mybir.dt.float32r
U32 = mybir.dt.uint32

P = 128
B, T, C = 8, 512, 512
KC = C // P
TT = T // P
H = 16
HD = 32
HG = P // HD
G = H // HG
EPS = 1e-5
TERMS = ((0, 0), (1, 0), (0, 1))


class Count:

    def __init__(self, ctx, nc, name, per_turn, credit=0):
        self.sem = ctx.enter_context(nc.semaphore(name))
        self.name, self.per_turn, self.credit, self.made = name, per_turn, credit, 0

    def at(self, turn, n):
        return turn * self.per_turn + (n + self.credit)


def split_sum(pe, out, stationary, moving, chunks):
    n, last = 0, None
    for k in chunks:
        for a, b in TERMS:
            last = pe.matmul(out, stationary(a, k), moving(b, k), start=(n == 0),
                             stop=(n == 3 * len(chunks) - 1))
            n += 1
    return last


def wait_apart(eng, sem, value, passed):
    eng.wait_ge(passed, 1)
    eng.wait_ge(sem, value)


def wait_by_memset(nc, sem, value, scratch):
    nc.vector.wait_ge(sem, value)
    nc.vector.memset(scratch, 0.0)


def cross_attention(nc, bank, x, ctx_in, w_kv, w_q, w_proj, b_proj, gate, x1_dram):
    SCALE = HD ** -0.5
    GROUP_DMAS = 2 * 3
    with ExitStack() as ctx:
        def sb(name, shape, dt=F32):
            return ctx.enter_context(nc.sbuf_tensor("a_" + name, shape, dt))

        def sem(name):
            return ctx.enter_context(nc.semaphore("a_" + name))

        def count(name, per_turn, credit=0):
            return Count(ctx, nc, "a_" + name, per_turn, credit)

        wq = sb("wq", [P, 2, KC, C], F32R)
        wk = sb("wk", [P, 2, KC, C], F32R)
        wv = sb("wv", [P, 2, KC, C], F32R)
        wp = sb("wp", [P, 2, KC, C], F32R)
        ident = sb("ident", [P, P])
        ones = sb("ones", [P, HD])
        bias = sb("bias", [P, C])
        tg = sb("tg", [P, 2])
        x_tok = sb("x_tok", [P, TT, C])
        ctx_tok = sb("ctx_tok", [P, TT, C])
        res = sb("res", [P, TT, C])
        ctxT = sb("ctxT", [P, 2, KC, T], F32R)
        xT = sb("xT", [P, 2, KC, T], F32R)
        oT = sb("oT", [P, 2, G, T], F32R)
        qk = sb("qk", [P, 2, 2, T], F32R)
        q_stack = sb("q_stack", [97, 2, HG, T], F32R)
        k_stack = sb("k_stack", [97, 2, HG, T], F32R)
        v = sb("v", [P, TT, C])
        prob = sb("prob", [P, 2, HG, T])
        xn = prob[:, 0]
        o_norm = sb("o_norm", [P, T])
        neg_max = sb("neg_max", [P, 2, HG * TT])
        max_row = sb("max_row", [HG * TT, 2, P], F32R)
        waited = sb("waited", [P, 1])
        st6 = sb("st6", [P, TT, 6])
        mv = sb("mv", [P, TT, 2])
        veps = sb("veps", [P, TT])
        mhalf = sb("mhalf", [P, TT])
        rstd = sb("rstd", [P, TT])

        w_in = [sem(f"w_in{n}") for n in range(5)]
        small_in = sem("small_in")
        w_main = sem("w_main")
        w_rest = sem("w_rest")
        ident_zero = sem("ident_zero")
        const_ready = sem("const_ready")
        fill_ready = sem("fill_ready")
        tg_ready = sem("tg_ready")
        bias_ready = sem("bias_ready")

        x_in = count("x_in", 16)
        ctx_load = count("ctx_load", 16)
        res_ready = count("res_ready", TT, 1)
        res_stored = count("res_stored", 16, 16)
        veps_ready = count("veps_ready", 1)
        rstd_ready = count("rstd_ready", 1)
        xn_ready = count("xn_ready", TT, 1)
        turned = count("turned", 2 * KC, 1)
        turned_main = count("turned_main", 2 * KC)
        turned_rest = count("turned_rest", 2 * KC)
        v_sum = count("v_sum", TT)
        v_ready = count("v_ready", TT)
        qk_sum = count("qk_sum", 2 * G)
        qk_main = count("qk_main", 2 * G)
        qk_rest = count("qk_rest", 2 * G)
        stack_in = [count(f"stack_in{s}", G // 2 * GROUP_DMAS * 16) for s in range(2)]
        max_sum = count("max_sum", H * TT)
        max_done = count("max_done", H * TT)
        max_turned = count("max_turned", G)
        row_ready = count("row_ready", G)
        row_in = [count(f"row_in{s}", G // 2 * 16) for s in range(2)]
        score_sum = count("score_sum", H * TT)
        exp_done = count("exp_done", H * TT)
        pv_done = count("pv_done", G * TT)
        recip_done = count("recip_done", G)
        o_ready = count("o_ready", G)
        o_main = count("o_main", G)
        o_rest = count("o_rest", G)
        proj_sum = count("proj_sum", TT)
        x1_ready = count("x1_ready", TT, TT)
        dve_step = count("dve_step", TT + 1)

        w_src = [w_q.rearrange("(k p) n -> p k n", p=P),
                 w_kv[:, 0:C].rearrange("(k p) n -> p k n", p=P),
                 w_kv[:, C:2 * C].rearrange("(k p) n -> p k n", p=P),
                 w_proj.rearrange("(k p) n -> p k n", p=P)]
        w_dst = [wq, wk, wv, wp]
        w_raw = [res, v, prob[:, 0], prob[:, 1]]
        x_src = x.rearrange("b (t p) c -> b p t c", p=P)
        ctx_src = ctx_in.rearrange("b (t p) c -> b p t c", p=P)
        x1_dst = x1_dram.rearrange("b (t p) c -> b p t c", p=P)

        def columns(n, w, placed=False):
            order = "p (g d h) -> p g h d" if placed and n < 2 else "p (g h d) -> p g h d"
            return w.rearrange(order, h=HG, d=HD)

        block = ctx.enter_context(nc.Block())

        @block.sync
        def _(sp):
            for n in (2, 0, 1, 3):
                sp.dma_start(w_raw[n][:], w_src[n]).then_inc(w_in[n], 16)
            sp.wait_ge(w_rest, 1)
            with sp.Fori(0, B) as i:
                wait_apart(sp, turned.sem, turned.at(i, 0), w_rest)
                sp.dma_start(ctx_tok[:], ctx_src[i]).then_inc(ctx_load.sem, 16)
                sp.wait_ge(xn_ready.sem, xn_ready.at(i, 0))
                wait_apart(sp, res_ready.sem, res_ready.at(i, 0), w_rest)
                sp.dma_start(x_tok[:], x_src[i]).then_inc(x_in.sem, 16)

                def stacks(g):
                    s = g % 2
                    for w, stack, parts in ((0, q_stack, (0, 0, 1)), (1, k_stack, (0, 1, 0))):
                        sp.wait_ge(qk_rest.sem, qk_rest.at(i, 2 * g + w + 1))
                        for piece, part in enumerate(parts):
                            sp.dma_start(stack[HD * piece:HD * (piece + 1), s, :, :].bitcast(F32),
                                         qk[:, w, part, :].bitcast(F32)).then_inc(stack_in[s].sem, 16)

                def row(g):
                    sp.wait_ge(row_ready.sem, row_ready.at(i, g + 1))
                    sp.dma_start(q_stack[96:97, g % 2, :, :].bitcast(F32),
                                 max_row[:, g % 2, :].bitcast(F32)).then_inc(row_in[g % 2].sem, 16)

                stacks(0)
                stacks(1)
                row(0)
                for g in range(1, G):
                    row(g)
                    if g + 1 < G:
                        stacks(g + 1)

        @block.gpsimd
        def _(pool):
            pool.dma_start(tg[:, 0:1], gate.partition_broadcast(P)).then_inc(small_in, 16)
            pool.dma_start(bias[:], b_proj.partition_broadcast(P)).then_inc(small_in, 16)
            nc.gpsimd.memset(ident[:], 0.0).then_inc(ident_zero, 1)
            pool.wait_ge(ident_zero, 1)
            nc.gpsimd.affine_select(out=ident[:], in_=ident[:], compare_op=ALU.not_equal, fill=1.0, base=0,
                                    pattern=[[-1, P]], channel_multiplier=1).then_inc(const_ready, 1)
            pool.wait_ge(tg_ready, 1)
            pool.wait_ge(fill_ready, 1)
            nc.gpsimd.tensor_scalar(bias[:], bias[:], tg[:, 1:2], 1.0, ALU.mult, ALU.mult).then_inc(bias_ready, 1)
            pool.wait_ge(bias_ready, 1)
            pool.wait_ge(w_rest, 4)
            pool.sem_inc(res_ready.sem, 1)
            with pool.Fori(0, B) as i:
                pool.wait_ge(veps_ready.sem, veps_ready.at(i, 1))
                nc.gpsimd.tensor_tensor(rstd[:], veps[:], mhalf[:], ALU.pow).then_inc(rstd_ready.sem, 1)
                pool.wait_ge(x_in.sem, x_in.at(i, 16))
                pool.wait_ge(res_stored.sem, res_stored.at(i, 0))
                for t in range(TT):
                    nc.gpsimd.tensor_tensor(res[:, t], x_tok[:, t], bias[:], ALU.add).then_inc(res_ready.sem, 1)
                for g in range(G):
                    pool.wait_ge(o_main.sem, o_main.at(i, g + 1))
                    nc.gpsimd.tensor_tensor(oT[:, 1, g, :], o_norm[:], oT[:, 0, g, :].bitcast(F32),
                                            ALU.subtract).then_inc(o_rest.sem, 1)

        @block.scalar
        def _(act):
            act.sem_inc(res_stored.sem, 16)
            act.wait_ge(small_in, 32)
            nc.scalar.activation(tg[:, 1:2], tg[:, 0:1], ACT.Tanh).then_inc(tg_ready, 1)
            for n in (2, 0, 1, 3):
                act.wait_ge(w_in[n], 16)
                for k in range(KC):
                    last = nc.scalar.activation(columns(n, w_dst[n][:, 0, k], True), columns(n, w_raw[n][:, k]),
                                                ACT.Copy)
                last.then_inc(w_main, 1)
            act.wait_ge(w_rest, 4)
            with act.Fori(0, B) as i:
                for n in range(2 * KC):
                    dst = (ctxT, xT)[n // KC][:, 0, n % KC, :]
                    act.wait_ge(turned.sem, turned.at(i, n + 1))
                    nc.scalar.activation(dst, bank[n], ACT.Copy).then_inc(turned_main.sem, 1)

                def qk_mains(g):
                    for w in range(2):
                        b = 4 + 2 * (g == 1) + w
                        act.wait_ge(qk_sum.sem, qk_sum.at(i, 2 * g + w + 1))
                        if g:
                            act.wait_ge(stack_in[(g - 1) % 2].sem,
                                        stack_in[(g - 1) % 2].at(i, GROUP_DMAS * 16 * ((g - 1) // 2 + 1)))
                        nc.scalar.activation(qk[:, w, 0, :], bank[b], ACT.Copy).then_inc(qk_main.sem, 1)

                qk_mains(0)
                qk_mains(1)
                for t in range(TT):
                    act.wait_ge(v_sum.sem, v_sum.at(i, t + 1))
                    nc.scalar.activation(v[:, t, :], bank[4 + t], ACT.Copy).then_inc(v_ready.sem, 1)
                for g in range(G):
                    for k in range(TT):
                        for h in range(HG):
                            n = (g * TT + k) * HG + h
                            act.wait_ge(score_sum.sem, score_sum.at(i, n + 1))
                            if n >= 2 * HG:
                                act.wait_ge(pv_done.sem, pv_done.at(i, n // HG - 1))
                            nc.scalar.activation(prob[:, k % 2, h, :], bank[h], ACT.Exp,
                                                 scale=SCALE).then_inc(exp_done.sem, 1)
                    act.wait_ge(o_ready.sem, o_ready.at(i, g + 1))
                    nc.scalar.activation(oT[:, 0, g, :], o_norm[:], ACT.Copy).then_inc(o_main.sem, 1)
                    if g + 2 < G:
                        qk_mains(g + 2)
                act.wait_ge(x1_ready.sem, x1_ready.at(i, TT))
                act.dma_start(x1_dst[i], res[:]).then_inc(res_stored.sem, 16)
            act.wait_ge(res_stored.sem, res_stored.at(B, 0))

        @block.vector
        def _(dve):
            nc.vector.memset(mhalf[:], -0.5).then_inc(fill_ready, 1)
            nc.vector.memset(ones[:], 1.0).then_inc(fill_ready, 1)
            nc.vector.memset(k_stack[96:97, :, :, :].bitcast(F32), 1.0).then_inc(fill_ready, 1)
            dve.sem_inc(xn_ready.sem, 1)
            dve.sem_inc(x1_ready.sem, TT)
            for n, src in enumerate((2, 0, 1, 3)):
                dve.wait_ge(w_main, n + 1)
                for k in range(KC):
                    last = nc.vector.tensor_tensor(columns(src, w_dst[src][:, 1, k], True),
                                                   columns(src, w_raw[src][:, k]),
                                                   columns(src, w_dst[src][:, 0, k].bitcast(F32), True), ALU.subtract)
                last.then_inc(w_rest, 1)
            with dve.Fori(0, B) as i:
                dve.wait_ge(x_in.sem, x_in.at(i, 16))
                for t in range(TT):
                    nc.vector.bn_stats(st6[:, t], x_tok[:, t]).then_inc(dve_step.sem, 1)
                wait_by_memset(nc, dve_step.sem, dve_step.at(i, TT), waited[:])
                for t in range(TT):
                    last = nc.vector.bn_aggr(mv[:, t], st6[:, t])
                last.then_inc(dve_step.sem, 1)
                dve.wait_ge(dve_step.sem, dve_step.at(i, TT + 1))
                nc.vector.tensor_scalar(veps[:], mv[:, :, 1], EPS, None, ALU.add).then_inc(veps_ready.sem, 1)

                def rests(n):
                    dst = (ctxT, xT)[n // KC][:, :, n % KC, :]
                    dve.wait_ge(turned_main.sem, turned_main.at(i, n + 1))
                    nc.vector.tensor_tensor(dst[:, 1], bank[n], dst[:, 0].bitcast(F32),
                                            ALU.subtract).then_inc(turned_rest.sem, 1)

                dve.wait_ge(rstd_ready.sem, rstd_ready.at(i, 1))
                for t in range(TT):
                    nc.vector.tensor_scalar(xn[:, t], x_tok[:, t], mv[:, t, 0:1], rstd[:, t:t + 1],
                                            ALU.subtract, ALU.mult).then_inc(xn_ready.sem, 1)
                for n in range(2 * KC):
                    rests(n)

                def qk_rests(g):
                    for w in range(2):
                        b = 4 + 2 * (g == 1) + w
                        dve.wait_ge(qk_main.sem, qk_main.at(i, 2 * g + w + 1))
                        nc.vector.tensor_tensor(qk[:, w, 1, :], bank[b], qk[:, w, 0, :].bitcast(F32),
                                                ALU.subtract).then_inc(qk_rest.sem, 1)

                def maxima(g, t):
                    for h in range(HG):
                        n = (g * TT + t) * HG + h
                        dve.wait_ge(max_sum.sem, max_sum.at(i, n + 1))
                        b = n % 4 if g == 0 else 4 + n % 2
                        nc.vector.tensor_reduce(neg_max[:, g % 2, h * TT + t:h * TT + t + 1], bank[b],
                                                AX_X, ALU.max, negate=True).then_inc(max_done.sem, 1)

                def rows(g):
                    dve.wait_ge(max_turned.sem, max_turned.at(i, g + 1))
                    nc.vector.tensor_copy(max_row[:, g % 2, :], bank[0][0:HG * TT, 0:P]).then_inc(row_ready.sem, 1)

                qk_rests(0)
                qk_rests(1)
                for t in range(TT):
                    maxima(0, t)
                rows(0)
                for g in range(G):
                    for k in range(TT):
                        if g + 1 < G:
                            maxima(g + 1, k)
                    if g + 1 < G:
                        rows(g + 1)
                    dve.wait_ge(pv_done.sem, pv_done.at(i, TT * (g + 1)))
                    if g:
                        dve.wait_ge(o_rest.sem, o_rest.at(i, g))
                    nc.vector.reciprocal(o_norm[:], bank[7]).then_inc(recip_done.sem, 1)
                    dve.wait_ge(recip_done.sem, recip_done.at(i, g + 1))
                    nc.vector.tensor_tensor(o_norm[:], bank[6], o_norm[:], ALU.mult).then_inc(o_ready.sem, 1)
                    if g + 2 < G:
                        qk_rests(g + 2)
                dve.wait_ge(res_ready.sem, res_ready.at(i, TT))
                for t in range(TT):
                    dve.wait_ge(proj_sum.sem, proj_sum.at(i, t + 1))
                    nc.vector.scalar_tensor_tensor(out=res[:, t], in0=bank[t], scalar=tg[:, 1:2], in1=res[:, t],
                                                   op0=ALU.mult, op1=ALU.add).then_inc(x1_ready.sem, 1)

        @block.tensor
        def _(pe):
            pe.wait_ge(const_ready, 1)
            pe.wait_ge(fill_ready, 3)
            pe.wait_ge(w_rest, 4)
            pe.sem_inc(turned.sem, 1)
            with pe.Fori(0, B) as i:
                def turn(src, n, ready, value):
                    for t in range(TT):
                        pe.wait_ge(ready, value(t))
                        last = pe.transpose(bank[n][:, t * P:(t + 1) * P],
                                            src[:, t, (n % KC) * P:(n % KC + 1) * P], ident[:])
                    last.then_inc(turned.sem, 1)

                for n in range(KC):
                    pe.wait_ge(x1_ready.sem, x1_ready.at(i, n + 1 - TT))
                    turn(ctx_tok, n, ctx_load.sem, lambda t: ctx_load.at(i, 16))
                for n in range(KC, 2 * KC):
                    turn(xn, n, xn_ready.sem, lambda t: xn_ready.at(i, t + 1))

                def project(g):
                    for w, weight, src in ((0, wq, xT), (1, wk, ctxT)):
                        b = 4 + 2 * (g == 1) + w
                        split_sum(pe, bank[b], lambda a, k: weight[:, a, k, g * P:(g + 1) * P],
                                  lambda a, k: src[:, a, k, :], range(KC)).then_inc(qk_sum.sem, 1)

                def max_scores(g, t, heads):
                    for h in heads:
                        n = (g * TT + t) * HG + h
                        b = n % 4 if g == 0 else 4 + n % 2
                        ring = 4 if g == 0 else 2
                        if n >= ring:
                            pe.wait_ge(max_done.sem, max_done.at(i, n + 1 - ring))
                        pe.matmul(bank[b], q_stack[0:96, g % 2, h, t * P:(t + 1) * P],
                                  k_stack[0:96, g % 2, h, :], start=True, stop=True).then_inc(max_sum.sem, 1)

                def turn_max(g):
                    pe.wait_ge(max_done.sem, max_done.at(i, (g + 1) * TT * HG))
                    if g:
                        pe.wait_ge(exp_done.sem, exp_done.at(i, g * TT * HG))
                    pe.transpose(bank[0][0:HG * TT, 0:P], neg_max[:, g % 2, :], ident[:]).then_inc(max_turned.sem, 1)

                def scores(g, k, heads):
                    for h in heads:
                        n = (g * TT + k) * HG + h
                        if n >= HG:
                            pe.wait_ge(exp_done.sem, exp_done.at(i, n + 1 - HG))
                        pe.matmul(bank[h], k_stack[:, g % 2, h, k * P:(k + 1) * P], q_stack[:, g % 2, h, :],
                                  start=True, stop=True).then_inc(score_sum.sem, 1)

                def weigh(g, k, sums):
                    if not sums:
                        pe.wait_ge(exp_done.sem, exp_done.at(i, (g * TT + k + 1) * HG))
                        if k == 0 and g:
                            pe.wait_ge(o_ready.sem, o_ready.at(i, g))
                    for h in range(HG):
                        out = bank[7 if sums else 6][HD * h:HD * (h + 1), :]
                        c = g * P + h * HD
                        last = pe.matmul(out, ones[:] if sums else v[:, k, c:c + HD], prob[:, k % 2, h, :],
                                         start=(k == 0), stop=(k == TT - 1))
                    if sums:
                        last.then_inc(pv_done.sem, 1)

                pe.wait_ge(turned_rest.sem, turned_rest.at(i, 2 * KC))
                project(0)
                project(1)
                pe.wait_ge(stack_in[0].sem, stack_in[0].at(i, GROUP_DMAS * 16))
                for t in range(TT):
                    max_scores(0, t, range(HG))
                pe.wait_ge(qk_rest.sem, qk_rest.at(i, 4))
                for t in range(TT):
                    split_sum(pe, bank[4 + t], lambda a, k: ctxT[:, a, k, t * P:(t + 1) * P],
                              lambda a, k: wv[:, a, k, :], range(KC)).then_inc(v_sum.sem, 1)
                turn_max(0)
                pe.wait_ge(v_ready.sem, v_ready.at(i, TT))
                pe.wait_ge(row_ready.sem, row_ready.at(i, 1))
                for g in range(G):
                    pe.wait_ge(row_in[g % 2].sem, row_in[g % 2].at(i, (g // 2 + 1) * 16))
                    for k in range(TT):
                        if k == 0 and g + 1 < G:
                            n = (g + 1) // 2 + 1
                            pe.wait_ge(stack_in[(g + 1) % 2].sem,
                                       stack_in[(g + 1) % 2].at(i, GROUP_DMAS * 16 * n))
                        for pair in ((0, 1), (2, 3)):
                            for h in pair:
                                scores(g, k, (h,))
                                if g + 1 < G:
                                    max_scores(g + 1, k, (h,))
                            if k:
                                weigh(g, k - 1, pair[0] == 2)
                    weigh(g, TT - 1, False)
                    weigh(g, TT - 1, True)
                    if g + 1 < G:
                        turn_max(g + 1)
                    if g + 2 < G:
                        project(g + 2)
                pe.wait_ge(o_rest.sem, o_rest.at(i, G))
                for t in range(TT):
                    split_sum(pe, bank[t], lambda a, k: oT[:, a, k, t * P:(t + 1) * P],
                              lambda a, k: wp[:, a, k, :], range(KC)).then_inc(proj_sum.sem, 1)


def self_attention_and_router(nc, bank, x1_dram, w_ln1, w_q, w_kva, w_kvb, w_o, w_ln2, w_gate, e_bias, gate,
                              angles, base_dram, xt_dram, comb_dram):
    D = 2 * HD
    SCALE = D ** -0.5
    R = w_kvb.shape[0]
    E = w_gate.shape[1]
    J = HD // 2
    BIG = -1e30
    GROUP_DMAS = 3 + 3 + 6
    ROPE_BANKS = ((7, 4), (1, 2))

    def qk_bank(g, w):
        return (5 if g < 2 else 4) + w

    with ExitStack() as ctx:
        def sb(name, shape, dt=F32):
            return ctx.enter_context(nc.sbuf_tensor("b_" + name, shape, dt))

        def sem(name):
            return ctx.enter_context(nc.semaphore("b_" + name))

        def count(name, per_turn, credit=0):
            return Count(ctx, nc, "b_" + name, per_turn, credit)

        wq = sb("wq", [P, 2, KC, H * D], F32R)
        wkva = sb("wkva", [P, 2, KC, P], F32R)
        wkvb_k = sb("wkvb_k", [R, 2, C], F32R)
        wkvb_v = sb("wkvb_v", [R, 2, C], F32R)
        wo = sb("wo", [P, 2, G, C], F32R)
        wgate = sb("wgate", [P, 2, KC, E], F32R)
        gate_raw = sb("gate_raw", [P, KC, E])
        w1 = sb("w1", [P, KC])
        w2 = sb("w2", [P, KC])
        ebias = sb("ebias", [P, E])
        expert = sb("expert", [P, E])
        ident = sb("ident", [P, P])
        ident_r = sb("ident_r", [P, P], F32R)
        mask_q = sb("mask_q", [P, P], F32R)
        mask_k = sb("mask_k", [P, P], F32R)
        ones = sb("ones", [P, HD])
        tg = sb("tg", [P, 2])
        cs = sb("cs", [P, 2, T])
        x_tok = sb("x_tok", [P, TT, C])
        hT = sb("hT", [P, 2, KC, T], F32R)
        oT = sb("oT", [P, 2, G, T], F32R)
        qk = sb("qk", [P, 2, 2, T], F32R)
        rope = sb("rope", [P, 2, 2, T], F32R)
        tmp = sb("tmp", [P, T])
        o_norm = sb("o_norm", [P, T])
        lat = sb("lat", [R, 2, T], F32R)
        q_stack = sb("q_stack", [97, 2, HG, T], F32R)
        k_stack = sb("k_stack", [97, 2, HG, T], F32R)
        qr_stack = sb("qr_stack", [96, 2, HG, T], F32R)
        kr_stack = sb("kr_stack", [96, T], F32R)
        v = sb("v", [P, TT, C])
        prob = sb("prob", [P, 2, HG, T])
        xn = prob[:, 0]
        y2 = v
        neg_max = sb("neg_max", [P, 2, HG * TT])
        max_row = sb("max_row", [HG * TT, 2, P], F32R)
        waited = sb("waited", [P, 1])
        st6 = sb("st6", [P, TT, 6])
        mv = sb("mv", [P, TT, 2])
        stat = sb("stat", [P, 6, TT])
        mhalf = sb("mhalf", [P, TT])
        ssq = sb("ssq", [P, 3, TT])
        logit = sb("logit", [P, TT, E])
        top = sb("top", [P, TT, 8])
        index = sb("index", [P, TT, 8], U32)
        index_f = sb("index_f", [P, TT, 8])
        pick = sb("pick", [P, 5, TT])
        one_hot = sb("one_hot", [P, 2, TT, E])
        comb = sb("comb", [P, TT, E])

        w_in = [sem(f"w_in{n}") for n in range(5)]
        w_main = sem("w_main")
        w_rest = sem("w_rest")
        small_in = sem("small_in")
        angles_in = sem("angles_in")
        kva_zero = sem("kva_zero")
        fill_ready = sem("fill_ready")
        mask_step = sem("mask_step")
        const_ready = sem("const_ready")
        tg_ready = sem("tg_ready")

        x_in = count("x_in", 16)
        stat_step = count("stat_step", TT + 4)
        var_ready = count("var_ready", 1)
        rstd_ready = count("rstd_ready", 1)
        ms_ready = count("ms_ready", 1)
        rms_ready = count("rms_ready", 1)
        h_ready = count("h_ready", TT)
        turned = count("turned", 2 * KC)
        turned_main = count("turned_main", 2 * KC)
        turned_rest = count("turned_rest", 2 * KC)
        lat_sum = count("lat_sum", 1)
        lat_main = count("lat_main", 3)
        lat_rest = count("lat_rest", 1)
        krope_step = count("krope_step", 6)
        krope_main = count("krope_main", 2)
        krope_rest = count("krope_rest", 2)
        csk_in = count("csk_in", 16)
        krope_in = count("krope_in", 6 * 16)
        v_sum = count("v_sum", TT)
        v_ready = count("v_ready", TT)
        qk_sum = count("qk_sum", 2 * G)
        qk_main = count("qk_main", 2 * G)
        qk_rest = count("qk_rest", 2 * G)
        rope_sum = count("rope_sum", 4)
        rope_step = count("rope_step", 2 * 6)
        rope_main = count("rope_main", 4)
        rope_rest = count("rope_rest", 4)
        stack_in = [count(f"stack_in{s}", G // 2 * GROUP_DMAS * 16) for s in range(2)]
        max_sum = count("max_sum", H * TT)
        max_done = count("max_done", H * TT)
        max_turned = count("max_turned", G)
        row_ready = count("row_ready", G)
        row_in = [count(f"row_in{s}", G // 2 * 16) for s in range(2)]
        score_sum = count("score_sum", H * TT)
        exp_done = count("exp_done", H * TT)
        pv_done = count("pv_done", G * TT)
        recip_done = count("recip_done", G)
        o_ready = count("o_ready", G)
        o_main = count("o_main", G)
        o_rest = count("o_rest", G)
        proj_sum = count("proj_sum", TT)
        y_step = count("y_step", 2 * TT)
        base_ready = count("base_ready", TT)
        square_done = count("square_done", TT)
        ssq_ready = count("ssq_ready", 1)
        rms2_ready = count("rms2_ready", 1)
        y_ready = count("y_ready", TT)
        logit_sum = count("logit_sum", 1)
        logit_read = count("logit_read", TT, TT)
        base_stored = count("base_stored", 16, 16)
        xt_stored = count("xt_stored", 16, 16)
        comb_stored = count("comb_stored", 16, 16)
        pick_step = count("pick_step", 8)
        diff_ready = count("diff_ready", 1)
        diff_exp = count("diff_exp", 1)
        comb_ready = count("comb_ready", 1)

        x_src = x1_dram.rearrange("b (t p) c -> b p t c", p=P)
        base_dst = base_dram.rearrange("b (t p) c -> b p t c", p=P)
        wq_src = w_q.rearrange("(k p) n -> p k n", p=P)
        wq_raw = [x_tok[:].rearrange("p (k x) c -> p k (x c)", k=2),
                  prob[:, 0].rearrange("p (k x) c -> p k (x c)", k=2)]
        wo_src = w_o.rearrange("(g h c) n -> g h c n", h=HG, c=D)
        kva_raw = prob[:, 1, 0, 0:KC * (R + HD)].rearrange("p (k n) -> p k n", k=KC)
        kvb_raw = prob[0:R, 1, 1, :]
        mask_raw = prob[:, 1, 2, 0:2 * P].rearrange("p (m c) -> p m c", m=2)
        csk = prob[0:J, 1, 0:2, :]

        def by_channel(w):
            return w.rearrange("p (g d h) -> p g h d", h=HG, d=HD)

        def by_head(w):
            return w.rearrange("p (g h d) -> p g h d", h=HG, d=HD)

        splits = [(0, wq_raw[0], wq[:, 0, 0:2], wq[:, 1, 0:2]),
                  (1, wq_raw[1], wq[:, 0, 2:4], wq[:, 1, 2:4]),
                  (2, v[:], wo[:, 0], wo[:, 1])]
        splits += [(3, kva_raw[:, :, a:b], wkva[:, 0, :, c:c + b - a], wkva[:, 1, :, c:c + b - a])
                   for a, b, c in ((0, R, 0), (R, R + J, R), (R + J, R + HD, 96))]
        splits += [(4, by_head(kvb_raw), by_channel(wkvb_k[:, 0]), by_channel(wkvb_k[:, 1])),
                   (4, kvb_raw, wkvb_v[:, 0], wkvb_v[:, 1]),
                   (4, gate_raw[:], wgate[:, 0], wgate[:, 1])]

        block = ctx.enter_context(nc.Block())

        @block.sync
        def _(sp):
            for n in range(2):
                sp.dma_start(wq_raw[n], wq_src[:, 2 * n:2 * n + 2, :]).then_inc(w_in[n], 16)
            for g in range(G):
                sp.dma_start(v[:, g, :], wo_src[g, :, 0:HD, :]).then_inc(w_in[2], 16)
            sp.dma_start(kva_raw, w_kva.rearrange("(k p) n -> p k n", p=P)).then_inc(w_in[3], 16)
            sp.dma_start(kvb_raw, w_kvb).then_inc(w_in[4], 16)
            sp.dma_start(gate_raw[:], w_gate.rearrange("(k p) n -> p k n", p=P)).then_inc(w_in[4], 16)
            sp.dma_start(cs[:], angles.rearrange("a p n -> p a n")).then_inc(angles_in, 16)
            sp.wait_ge(w_rest, len(splits))
            sp.wait_ge(fill_ready, 4)
            with sp.Fori(0, B) as i:
                wait_apart(sp, base_stored.sem, base_stored.at(i, 0), w_rest)
                sp.dma_start(x_tok[:], x_src[i]).then_inc(x_in.sem, 16)
                sp.wait_ge(comb_stored.sem, comb_stored.at(i, 0))
                sp.dma_start(csk, angles[:, 0:P // 2:HG, :].rearrange("a p n -> p a n")).then_inc(csk_in.sem, 16)
                sp.wait_ge(krope_rest.sem, krope_rest.at(i, 2))
                for e in range(2):
                    for piece, part in enumerate((0, 1, 0)):
                        row0 = HD * piece + J * e
                        sp.dma_start(kr_stack[row0:row0 + J, :].bitcast(F32),
                                     rope[0:J, e, part, :].bitcast(F32)).then_inc(krope_in.sem, 16)

                def stacks(g):
                    s = g % 2

                    def pieces(w, stack, parts):
                        sp.wait_ge(qk_rest.sem, qk_rest.at(i, 2 * g + w + 1))
                        for piece, part in enumerate(parts):
                            sp.dma_start(stack[HD * piece:HD * (piece + 1), s, :, :].bitcast(F32),
                                         qk[:, w, part, :].bitcast(F32)).then_inc(stack_in[s].sem, 16)

                    def rotated():
                        sp.wait_ge(rope_rest.sem, rope_rest.at(i, 2 * (g // 2) + 2))
                        for e in range(2):
                            for piece, part in enumerate((0, 0, 1)):
                                row0 = HD * piece + J * e
                                sp.dma_start(qr_stack[row0:row0 + J, s, :, :].bitcast(F32),
                                             rope[64 * s:64 * (s + 1), e, part, :].bitcast(F32)
                                             ).then_inc(stack_in[s].sem, 16)

                    pieces(0, q_stack, (0, 0, 1))
                    rotated()
                    pieces(1, k_stack, (0, 1, 0))

                def row(g):
                    sp.wait_ge(row_ready.sem, row_ready.at(i, g + 1))
                    sp.dma_start(q_stack[96:97, g % 2, :, :].bitcast(F32),
                                 max_row[:, g % 2, :].bitcast(F32)).then_inc(row_in[g % 2].sem, 16)

                stacks(0)
                stacks(1)
                row(0)
                for g in range(1, G):
                    row(g)
                    if g + 1 < G:
                        stacks(g + 1)
                wait_apart(sp, base_ready.sem, base_ready.at(i, TT), w_rest)
                sp.dma_start(base_dst[i], x_tok[:]).then_inc(base_stored.sem, 16)
                wait_apart(sp, turned_rest.sem, turned_rest.at(i, 2 * KC), w_rest)
                sp.dma_start(xt_dram[i], hT[:].bitcast(F32)).then_inc(xt_stored.sem, 16)
                wait_apart(sp, comb_ready.sem, comb_ready.at(i, 1), w_rest)
                sp.dma_start(comb_dram[i], comb[:]).then_inc(comb_stored.sem, 16)
            sp.wait_ge(base_stored.sem, base_stored.at(B, 0))
            sp.wait_ge(xt_stored.sem, xt_stored.at(B, 0))
            sp.wait_ge(comb_stored.sem, comb_stored.at(B, 0))

        @block.gpsimd
        def _(pool):
            for dst, src in ((tg[:, 0:1], gate.partition_broadcast(P)), (ebias[:], e_bias.partition_broadcast(P)),
                             (w1[:], w_ln1),
                             (w2[:], w_ln2)):
                pool.dma_start(dst, src).then_inc(small_in, 16)
            nc.gpsimd.iota(expert[:], pattern=[[1, E]], base=0, channel_multiplier=0,
                           allow_small_or_imprecise_dtypes=True).then_inc(mask_step, 1)
            pool.wait_ge(mask_step, 1)
            nc.gpsimd.memset(ident[:], 0.0).then_inc(mask_step, 1)
            pool.wait_ge(mask_step, 2)
            nc.gpsimd.memset(mask_raw, 0.0).then_inc(mask_step, 1)
            pool.wait_ge(mask_step, 3)
            nc.gpsimd.affine_select(out=ident[:], in_=ident[:], compare_op=ALU.not_equal, fill=1.0, base=0,
                                    pattern=[[-1, P]], channel_multiplier=1).then_inc(mask_step, 1)
            pool.wait_ge(mask_step, 4)
            nc.gpsimd.affine_select(out=mask_raw[:, 0], in_=mask_raw[:, 0], compare_op=ALU.is_ge, fill=BIG, base=0,
                                    pattern=[[-1, P]], channel_multiplier=1).then_inc(mask_step, 1)
            pool.wait_ge(mask_step, 5)
            nc.gpsimd.affine_select(out=mask_raw[:, 1], in_=mask_raw[:, 1], compare_op=ALU.is_ge, fill=BIG, base=0,
                                    pattern=[[1, P]], channel_multiplier=-1).then_inc(const_ready, 1)
            pool.wait_ge(fill_ready, 1)
            pool.sem_inc(base_stored.sem, 16)
            pool.sem_inc(xt_stored.sem, 16)
            pool.sem_inc(comb_stored.sem, 16)
            with pool.Fori(0, B) as i:
                pool.wait_ge(var_ready.sem, var_ready.at(i, 1))
                nc.gpsimd.tensor_tensor(stat[:, 1], stat[:, 0], mhalf[:], ALU.pow).then_inc(rstd_ready.sem, 1)
                pool.wait_ge(ms_ready.sem, ms_ready.at(i, 1))
                nc.gpsimd.tensor_tensor(stat[:, 4], stat[:, 3], mhalf[:], ALU.pow).then_inc(rms_ready.sem, 1)
                for g in range(G):
                    pool.wait_ge(o_main.sem, o_main.at(i, g + 1))
                    nc.gpsimd.tensor_tensor(oT[:, 1, g, :], o_norm[:], oT[:, 0, g, :].bitcast(F32),
                                            ALU.subtract).then_inc(o_rest.sem, 1)
                pool.wait_ge(ssq_ready.sem, ssq_ready.at(i, 1))
                nc.gpsimd.tensor_tensor(ssq[:, 2], ssq[:, 1], mhalf[:], ALU.pow).then_inc(rms2_ready.sem, 1)

        @block.scalar
        def _(act):
            act.wait_ge(small_in, 4 * 16)
            nc.scalar.activation(tg[:, 1:2], tg[:, 0:1], ACT.Tanh).then_inc(tg_ready, 1)
            act.wait_ge(kva_zero, 1)
            for n, raw, main, _ in splits:
                act.wait_ge(w_in[n], (16, 16, 64, 16, 32)[n])
                nc.scalar.activation(main, raw, ACT.Copy).then_inc(w_main, 1)
            with act.Fori(0, B) as i:
                act.wait_ge(xt_stored.sem, xt_stored.at(i, 0))

                def turn_mains(first, b, w):
                    for k in range(KC):
                        act.wait_ge(turned.sem, turned.at(i, first + k + 1))
                        nc.scalar.activation(hT[:, 0, k, :], bank[b + k], ACT.Copy,
                                             scale=w[:, k:k + 1]).then_inc(turned_main.sem, 1)

                def qk_main_of(g, w):
                    act.wait_ge(qk_sum.sem, qk_sum.at(i, 2 * g + w + 1))
                    if g:
                        act.wait_ge(stack_in[(g - 1) % 2].sem,
                                    stack_in[(g - 1) % 2].at(i, GROUP_DMAS * 16 * ((g - 1) // 2 + 1)))
                    nc.scalar.activation(qk[:, w, 0, :], bank[qk_bank(g, w)], ACT.Copy).then_inc(qk_main.sem, 1)

                def rope_mains(n):
                    if n:
                        for s in range(2):
                            act.wait_ge(stack_in[s].sem, stack_in[s].at(i, GROUP_DMAS * 16))
                    else:
                        act.wait_ge(krope_in.sem, krope_in.at(i, 6 * 16))
                    for e in range(2):
                        act.wait_ge(rope_step.sem, rope_step.at(i, 6 * n + (3, 6)[e]))
                        nc.scalar.activation(rope[:, e, 0, :], tmp[:], ACT.Copy).then_inc(rope_main.sem, 1)

                turn_mains(0, 0, w1)
                act.wait_ge(lat_sum.sem, lat_sum.at(i, 1))
                nc.scalar.activation(lat[:, 0, :], bank[4][0:R], ACT.Copy).then_inc(lat_main.sem, 1)
                nc.scalar.activation(v[0:J, 0, :], bank[4][R:R + J], ACT.Copy).then_inc(lat_main.sem, 1)
                nc.scalar.activation(v[0:J, 1, :], bank[4][96:96 + J], ACT.Copy).then_inc(lat_main.sem, 1)
                for e in range(2):
                    act.wait_ge(krope_step.sem, krope_step.at(i, (3, 6)[e]))
                    nc.scalar.activation(rope[0:J, e, 0, :], v[0:J, 2, :], ACT.Copy).then_inc(krope_main.sem, 1)
                qk_main_of(0, 0)
                rope_mains(0)
                qk_main_of(0, 1)
                qk_main_of(1, 0)
                qk_main_of(1, 1)
                for t in range(TT):
                    act.wait_ge(v_sum.sem, v_sum.at(i, t + 1))
                    nc.scalar.activation(v[:, t, :], bank[4 + t], ACT.Copy).then_inc(v_ready.sem, 1)
                for g in range(G):
                    for k in range(TT):
                        for h in range(HG):
                            n = (g * TT + k) * HG + h
                            act.wait_ge(score_sum.sem, score_sum.at(i, n + 1))
                            if n >= 2 * HG:
                                act.wait_ge(pv_done.sem, pv_done.at(i, n // HG - 1))
                            nc.scalar.activation(prob[:, k % 2, h, k * P:], bank[h][:, 0:T - k * P], ACT.Exp,
                                                 scale=SCALE).then_inc(exp_done.sem, 1)
                    act.wait_ge(o_ready.sem, o_ready.at(i, g + 1))
                    nc.scalar.activation(oT[:, 0, g, :], o_norm[:], ACT.Copy).then_inc(o_main.sem, 1)
                    if g == 0:
                        rope_mains(1)
                    if g + 2 < G:
                        for w in range(2):
                            qk_main_of(g + 2, w)
                for t in range(TT):
                    act.wait_ge(y_step.sem, y_step.at(i, TT + t + 1))
                    nc.scalar.activation(prob[:, 1, t, :], y2[:, t], ACT.Square,
                                         accum_out=ssq[:, 0, t:t + 1]).then_inc(square_done.sem, 1)
                turn_mains(KC, 4, w2)
                act.wait_ge(diff_ready.sem, diff_ready.at(i, 1))
                nc.scalar.activation(pick[:, 1], pick[:, 0], ACT.Exp).then_inc(diff_exp.sem, 1)

        @block.vector
        def _(dve):
            nc.vector.memset(mhalf[:], -0.5).then_inc(fill_ready, 1)
            nc.vector.memset(ones[:], 1.0).then_inc(fill_ready, 1)
            nc.vector.memset(wkva[:].bitcast(F32), 0.0).then_inc(kva_zero, 1)
            nc.vector.memset(k_stack[96:97, :, :, :].bitcast(F32), 1.0).then_inc(fill_ready, 1)
            dve.wait_ge(kva_zero, 1)
            for n, (_, raw, main, rest) in enumerate(splits):
                dve.wait_ge(w_main, n + 1)
                nc.vector.tensor_tensor(rest, raw, main.bitcast(F32), ALU.subtract).then_inc(w_rest, 1)
            dve.wait_ge(const_ready, 1)
            dve.wait_ge(tg_ready, 1)
            dve.wait_ge(angles_in, 16)
            nc.vector.tensor_copy(ident_r[:], ident[:])
            nc.vector.tensor_copy(mask_q[:], mask_raw[:, 0])
            nc.vector.tensor_copy(mask_k[:], mask_raw[:, 1]).then_inc(fill_ready, 1)
            dve.sem_inc(logit_read.sem, TT)
            with dve.Fori(0, B) as i:
                steps = [0]

                def stat_of(ins, sem=None):
                    steps[0] += 1
                    ins.then_inc(stat_step.sem, 1)
                    dve.wait_ge(stat_step.sem, stat_step.at(i, steps[0]))

                dve.wait_ge(x_in.sem, x_in.at(i, 16))
                for t in range(TT):
                    nc.vector.bn_stats(st6[:, t], x_tok[:, t]).then_inc(stat_step.sem, 1)
                steps[0] = TT
                wait_by_memset(nc, stat_step.sem, stat_step.at(i, TT), waited[:])
                for t in range(TT - 1):
                    nc.vector.bn_aggr(mv[:, t], st6[:, t])
                stat_of(nc.vector.bn_aggr(mv[:, TT - 1], st6[:, TT - 1]))
                nc.vector.tensor_scalar(stat[:, 0], mv[:, :, 1], EPS, None, ALU.add).then_inc(var_ready.sem, 1)
                dve.wait_ge(rstd_ready.sem, rstd_ready.at(i, 1))
                stat_of(nc.vector.tensor_tensor(stat[:, 2], stat[:, 1], stat[:, 1], ALU.mult))
                stat_of(nc.vector.tensor_tensor(stat[:, 3], stat[:, 2], mv[:, :, 1], ALU.mult))
                nc.vector.tensor_scalar(stat[:, 3], stat[:, 3], EPS, None, ALU.add).then_inc(ms_ready.sem, 1)
                dve.wait_ge(rms_ready.sem, rms_ready.at(i, 1))
                stat_of(nc.vector.tensor_tensor(stat[:, 5], stat[:, 1], stat[:, 4], ALU.mult))
                for t in range(TT):
                    nc.vector.tensor_scalar(xn[:, t], x_tok[:, t], mv[:, t, 0:1], stat[:, 5, t:t + 1],
                                            ALU.subtract, ALU.mult).then_inc(h_ready.sem, 1)

                def turn_rests(first, b, w):
                    for k in range(KC):
                        dve.wait_ge(turned_main.sem, turned_main.at(i, first + k + 1))
                        nc.vector.scalar_tensor_tensor(out=hT[:, 1, k, :], in0=bank[b + k], scalar=w[:, k:k + 1],
                                                       in1=hT[:, 0, k, :].bitcast(F32), op0=ALU.mult,
                                                       op1=ALU.subtract).then_inc(turned_rest.sem, 1)

                def rotate(even, odd, cos, sin, res, aux, step, at, main_ready, dst, rest_done):
                    nc.vector.tensor_tensor(res, even, cos, ALU.mult).then_inc(step.sem, 1)
                    nc.vector.tensor_tensor(aux, odd, sin, ALU.mult).then_inc(step.sem, 1)
                    dve.wait_ge(step.sem, step.at(i, at + 2))
                    nc.vector.tensor_tensor(res, res, aux, ALU.subtract).then_inc(step.sem, 1)
                    dve.wait_ge(step.sem, step.at(i, at + 3))
                    nc.vector.tensor_tensor(aux, even, sin, ALU.mult).then_inc(step.sem, 1)
                    main_ready(0)
                    nc.vector.tensor_tensor(dst(0, 1), res, dst(0, 0).bitcast(F32),
                                            ALU.subtract).then_inc(rest_done.sem, 1)
                    dve.wait_ge(rest_done.sem, rest_done.at(i, 2 * (at // 6) + 1))
                    nc.vector.tensor_tensor(res, odd, cos, ALU.mult).then_inc(step.sem, 1)
                    dve.wait_ge(step.sem, step.at(i, at + 5))
                    nc.vector.tensor_tensor(res, res, aux, ALU.add).then_inc(step.sem, 1)
                    dve.wait_ge(step.sem, step.at(i, at + 6))
                    main_ready(1)
                    nc.vector.tensor_tensor(dst(1, 1), res, dst(1, 0).bitcast(F32),
                                            ALU.subtract).then_inc(rest_done.sem, 1)
                    dve.wait_ge(rest_done.sem, rest_done.at(i, 2 * (at // 6) + 2))

                def rope_of(n):
                    dve.wait_ge(rope_sum.sem, rope_sum.at(i, 2 * n + 2))
                    if n:
                        dve.wait_ge(o_rest.sem, o_rest.at(i, 1))
                    rotate(bank[ROPE_BANKS[n][0]], bank[ROPE_BANKS[n][1]], cs[:, 0], cs[:, 1], tmp[:], o_norm[:],
                           rope_step, 6 * n,
                           lambda e: dve.wait_ge(rope_main.sem, rope_main.at(i, 2 * n + e + 1)),
                           lambda e, part: rope[:, e, part, :], rope_rest)

                def qk_rest_of(g, w):
                    dve.wait_ge(qk_main.sem, qk_main.at(i, 2 * g + w + 1))
                    nc.vector.tensor_tensor(qk[:, w, 1, :], bank[qk_bank(g, w)], qk[:, w, 0, :].bitcast(F32),
                                            ALU.subtract).then_inc(qk_rest.sem, 1)

                def maxima(g, t):
                    for h in range(HG):
                        n = (g * TT + t) * HG + h
                        dve.wait_ge(max_sum.sem, max_sum.at(i, n + 1))
                        b = n % 4 if g == 0 else 4 + n % 2
                        nc.vector.tensor_reduce(neg_max[:, g % 2, h * TT + t:h * TT + t + 1],
                                                bank[b][:, 0:(t + 1) * P], AX_X, ALU.max,
                                                negate=True).then_inc(max_done.sem, 1)

                def rows(g):
                    dve.wait_ge(max_turned.sem, max_turned.at(i, g + 1))
                    nc.vector.tensor_copy(max_row[:, g % 2, :], bank[0][0:HG * TT, 0:P]).then_inc(row_ready.sem, 1)

                turn_rests(0, 0, w1)
                dve.wait_ge(lat_main.sem, lat_main.at(i, 1))
                nc.vector.tensor_tensor(lat[:, 1, :], bank[4][0:R], lat[:, 0, :].bitcast(F32),
                                        ALU.subtract).then_inc(lat_rest.sem, 1)
                dve.wait_ge(lat_main.sem, lat_main.at(i, 3))
                dve.wait_ge(csk_in.sem, csk_in.at(i, 16))
                rotate(v[0:J, 0, :], v[0:J, 1, :], csk[:, 0], csk[:, 1], v[0:J, 2, :], v[0:J, 3, :], krope_step, 0,
                       lambda e: dve.wait_ge(krope_main.sem, krope_main.at(i, e + 1)),
                       lambda e, part: rope[0:J, e, part, :], krope_rest)
                qk_rest_of(0, 0)
                dve.wait_ge(krope_in.sem, krope_in.at(i, 6 * 16))
                rope_of(0)
                qk_rest_of(0, 1)
                qk_rest_of(1, 0)
                qk_rest_of(1, 1)
                for t in range(TT):
                    maxima(0, t)
                rows(0)
                for g in range(G):
                    if g + 1 < G:
                        for t in range(TT):
                            maxima(g + 1, t)
                        rows(g + 1)
                    dve.wait_ge(pv_done.sem, pv_done.at(i, TT * (g + 1)))
                    if g:
                        dve.wait_ge(o_rest.sem, o_rest.at(i, g))
                    nc.vector.reciprocal(o_norm[:], bank[7]).then_inc(recip_done.sem, 1)
                    dve.wait_ge(recip_done.sem, recip_done.at(i, g + 1))
                    nc.vector.tensor_tensor(o_norm[:], bank[6], o_norm[:], ALU.mult).then_inc(o_ready.sem, 1)
                    if g == 0:
                        rope_of(1)
                    if g + 2 < G:
                        for w in range(2):
                            qk_rest_of(g + 2, w)
                for t in range(TT):
                    nc.vector.tensor_scalar(y2[:, t], x_tok[:, t], mv[:, t, 0:1], stat[:, 1, t:t + 1],
                                            ALU.subtract, ALU.mult).then_inc(y_step.sem, 1)
                for t in range(TT):
                    dve.wait_ge(proj_sum.sem, proj_sum.at(i, t + 1))
                    if t == 0:
                        dve.wait_ge(y_step.sem, y_step.at(i, TT))
                    nc.vector.tensor_tensor(y2[:, t], bank[t], y2[:, t], ALU.add).then_inc(y_step.sem, 1)
                for t in range(TT):
                    dve.wait_ge(y_step.sem, y_step.at(i, TT + t + 1))
                    nc.vector.scalar_tensor_tensor(out=x_tok[:, t], in0=y2[:, t], scalar=tg[:, 1:2],
                                                   in1=x_tok[:, t], op0=ALU.mult,
                                                   op1=ALU.add).then_inc(base_ready.sem, 1)
                dve.wait_ge(square_done.sem, square_done.at(i, TT))
                nc.vector.tensor_scalar(ssq[:, 1], ssq[:, 0], 1.0 / C, EPS, ALU.mult,
                                        ALU.add).then_inc(ssq_ready.sem, 1)
                dve.wait_ge(rms2_ready.sem, rms2_ready.at(i, 1))
                dve.wait_ge(base_ready.sem, base_ready.at(i, TT))
                for t in range(TT):
                    nc.vector.tensor_scalar(y2[:, t], y2[:, t], ssq[:, 2, t:t + 1], None,
                                            ALU.mult).then_inc(y_ready.sem, 1)
                turn_rests(KC, 4, w2)

                picks = [0]

                def pick_of(ins):
                    picks[0] += 1
                    ins.then_inc(pick_step.sem, 1)
                    wait_by_memset(nc, pick_step.sem, pick_step.at(i, picks[0]), waited[:])

                dve.wait_ge(logit_sum.sem, logit_sum.at(i, 1))
                for t in range(TT):
                    nc.vector.tensor_tensor(logit[:, t], bank[0][:, t * E:(t + 1) * E], ebias[:],
                                            ALU.add).then_inc(logit_read.sem, 1)
                wait_by_memset(nc, logit_read.sem, logit_read.at(i, TT), waited[:])
                for t in range(TT):
                    last = nc.vector.max(top[:, t], logit[:, t])
                pick_of(last)
                for t in range(TT):
                    last = nc.vector.max_index(index[:, t], top[:, t], logit[:, t])
                pick_of(last)
                pick_of(nc.vector.tensor_copy(index_f[:], index[:]))
                nc.vector.tensor_tensor(pick[:, 0], top[:, :, 1], top[:, :, 0], ALU.subtract
                                        ).then_inc(diff_ready.sem, 1)
                dve.wait_ge(diff_exp.sem, diff_exp.at(i, 1))
                pick_of(nc.vector.tensor_scalar(pick[:, 2], pick[:, 1], 1.0, None, ALU.add))
                pick_of(nc.vector.reciprocal(pick[:, 2], pick[:, 2]))
                pick_of(nc.vector.tensor_scalar(pick[:, 3], pick[:, 2], tg[:, 1:2], None, ALU.mult))
                pick_of(nc.vector.tensor_tensor(pick[:, 4], pick[:, 3], pick[:, 1], ALU.mult))
                for t in range(TT):
                    for r in range(2):
                        last = nc.vector.tensor_scalar(one_hot[:, r, t], expert[:], index_f[:, t, r:r + 1],
                                                       pick[:, 3 + r, t:t + 1], ALU.is_equal, ALU.mult)
                pick_of(last)
                dve.wait_ge(comb_stored.sem, comb_stored.at(i, 0))
                nc.vector.tensor_tensor(comb[:], one_hot[:, 0], one_hot[:, 1], ALU.add).then_inc(comb_ready.sem, 1)

        @block.tensor
        def _(pe):
            pe.wait_ge(const_ready, 1)
            pe.wait_ge(fill_ready, 4)
            pe.wait_ge(w_rest, len(splits))
            with pe.Fori(0, B) as i:
                def turn(src, k, b, ready):
                    for t in range(TT):
                        pe.wait_ge(ready.sem, ready.at(i, t + 1))
                        last = pe.transpose(bank[b + k][:, t * P:(t + 1) * P], src[:, t, k * P:(k + 1) * P], ident[:])
                    last.then_inc(turned.sem, 1)

                def project(b, columns, done):
                    split_sum(pe, bank[b], lambda a, k: wq[:, a, k, columns:columns + P],
                              lambda a, k: hT[:, a, k, :], range(KC)).then_inc(done.sem, 1)

                def project_k(g):
                    split_sum(pe, bank[qk_bank(g, 1)], lambda a, k: wkvb_k[:, a, g * P:(g + 1) * P],
                              lambda a, k: lat[:, a, :], range(1)).then_inc(qk_sum.sem, 1)

                def project_rope(n):
                    for e in range(2):
                        project(ROPE_BANKS[n][e], C + (2 * n + e) * P, rope_sum)

                def max_scores(g, t, heads):
                    for h in heads:
                        n = (g * TT + t) * HG + h
                        b = n % 4 if g == 0 else 4 + n % 2
                        ring = 4 if g == 0 else 2
                        if n >= ring:
                            pe.wait_ge(max_done.sem, max_done.at(i, n + 1 - ring))
                        s, w = g % 2, (t + 1) * P
                        pe.matmul(bank[b][:, 0:w], q_stack[0:96, s, h, t * P:w], k_stack[0:96, s, h, 0:w],
                                  start=True, stop=False)
                        pe.matmul(bank[b][:, t * P:w], ident_r[:], mask_q[:], start=False, stop=False)
                        pe.matmul(bank[b][:, 0:w], qr_stack[:, s, h, t * P:w], kr_stack[:, 0:w],
                                  start=False, stop=True).then_inc(max_sum.sem, 1)

                def turn_max(g):
                    pe.wait_ge(max_done.sem, max_done.at(i, (g + 1) * TT * HG))
                    if g:
                        pe.wait_ge(exp_done.sem, exp_done.at(i, g * TT * HG))
                    pe.transpose(bank[0][0:HG * TT, 0:P], neg_max[:, g % 2, :], ident[:]).then_inc(max_turned.sem, 1)

                def scores(g, k, h):
                    n = (g * TT + k) * HG + h
                    if n >= HG:
                        pe.wait_ge(exp_done.sem, exp_done.at(i, n + 1 - HG))
                    s, w = g % 2, T - k * P
                    pe.matmul(bank[h][:, 0:w], k_stack[:, s, h, k * P:(k + 1) * P], q_stack[:, s, h, k * P:],
                              start=True, stop=False)
                    pe.matmul(bank[h][:, 0:P], ident_r[:], mask_k[:], start=False, stop=False)
                    pe.matmul(bank[h][:, 0:w], kr_stack[:, k * P:(k + 1) * P], qr_stack[:, s, h, k * P:],
                              start=False, stop=True).then_inc(score_sum.sem, 1)

                def weigh(g, k, sums):
                    if not sums:
                        pe.wait_ge(exp_done.sem, exp_done.at(i, (g * TT + k + 1) * HG))
                        if k == 0 and g:
                            pe.wait_ge(o_ready.sem, o_ready.at(i, g))
                    for h in range(HG):
                        out = bank[7 if sums else 6][HD * h:HD * (h + 1), k * P:]
                        c = g * P + h * HD
                        last = pe.matmul(out, ones[:] if sums else v[:, k, c:c + HD], prob[:, k % 2, h, k * P:],
                                         start=(k == 0), stop=(k == TT - 1))
                    if sums:
                        last.then_inc(pv_done.sem, 1)

                pe.wait_ge(logit_read.sem, logit_read.at(i, 0))
                for k in range(KC):
                    turn(xn, k, 0, h_ready)
                pe.wait_ge(turned_rest.sem, turned_rest.at(i, KC))
                split_sum(pe, bank[4], lambda a, k: wkva[:, a, k, :], lambda a, k: hT[:, a, k, :],
                          range(KC)).then_inc(lat_sum.sem, 1)
                project(qk_bank(0, 0), 0, qk_sum)
                pe.wait_ge(lat_rest.sem, lat_rest.at(i, 1))
                pe.wait_ge(lat_main.sem, lat_main.at(i, 3))
                project_rope(0)
                project_k(0)
                pe.wait_ge(qk_rest.sem, qk_rest.at(i, 1))
                project(qk_bank(1, 0), P, qk_sum)
                pe.wait_ge(qk_rest.sem, qk_rest.at(i, 2))
                project_k(1)
                pe.wait_ge(stack_in[0].sem, stack_in[0].at(i, GROUP_DMAS * 16))
                pe.wait_ge(krope_in.sem, krope_in.at(i, 6 * 16))
                for t in range(TT):
                    max_scores(0, t, range(HG))
                pe.wait_ge(qk_rest.sem, qk_rest.at(i, 4))
                for t in range(TT):
                    split_sum(pe, bank[4 + t], lambda a, k: lat[:, a, t * P:(t + 1) * P],
                              lambda a, k: wkvb_v[:, a, :], range(1)).then_inc(v_sum.sem, 1)
                turn_max(0)
                pe.wait_ge(v_ready.sem, v_ready.at(i, TT))
                for g in range(G):
                    pe.wait_ge(row_in[g % 2].sem, row_in[g % 2].at(i, (g // 2 + 1) * 16))
                    if g + 1 < G:
                        pe.wait_ge(stack_in[(g + 1) % 2].sem,
                                   stack_in[(g + 1) % 2].at(i, GROUP_DMAS * 16 * ((g + 1) // 2 + 1)))
                    for k in range(TT):
                        for pair in ((0, 1), (2, 3)):
                            for h in pair:
                                scores(g, k, h)
                                if g + 1 < G:
                                    max_scores(g + 1, k, (h,))
                            if k:
                                weigh(g, k - 1, pair[0] == 2)
                    weigh(g, TT - 1, False)
                    weigh(g, TT - 1, True)
                    if g + 1 < G:
                        turn_max(g + 1)
                    if g == 0:
                        project_rope(1)
                    if g + 2 < G:
                        project(qk_bank(g + 2, 0), (g + 2) * P, qk_sum)
                        project_k(g + 2)
                    if g == 0:
                        pe.wait_ge(rope_rest.sem, rope_rest.at(i, 4))
                pe.wait_ge(o_rest.sem, o_rest.at(i, G))
                for t in range(TT):
                    split_sum(pe, bank[t], lambda a, k: oT[:, a, k, t * P:(t + 1) * P],
                              lambda a, k: wo[:, a, k, :], range(G)).then_inc(proj_sum.sem, 1)
                for k in range(KC):
                    turn(y2, k, 4, y_ready)
                pe.wait_ge(turned_rest.sem, turned_rest.at(i, 2 * KC))
                for t in range(TT):
                    last = split_sum(pe, bank[0][:, t * E:(t + 1) * E], lambda a, k: hT[:, a, k, t * P:(t + 1) * P],
                                     lambda a, k: wgate[:, a, k, :], range(KC))
                last.then_inc(logit_sum.sem, 1)


def experts(nc, banks, base_dram, xt_dram, comb_dram, w_gate, w_up, w_down, s_gate, s_up, s_down, gate, out):
    E, _, I = w_gate.shape
    S = s_gate.shape[0]
    IC = I // P
    HALVES = 2
    NB = B // HALVES
    STEPS = HALVES * (E + S)
    W = 2 * KC * I + IC * C
    assert S == 1 and E % 2 == 0
    with ExitStack() as ctx:
        def sb(name, shape, dt=F32):
            return ctx.enter_context(nc.sbuf_tensor("c_" + name, shape, dt))

        def count(name, per_step, credit=0):
            return Count(ctx, nc, "c_" + name, per_step, credit)

        xT = sb("xT", [P, NB, 2, KC, T], F32R)
        acc = sb("acc", [P, NB, TT, C])
        raw = sb("raw", [P, W])
        weights = sb("weights", [P, 2, 2, W], F32R)
        silu = sb("silu", [P, IC, T])
        hidden = sb("hidden", [P, IC, T])
        hT = sb("hT", [P, 2, 2, IC, T], F32R)
        comb = sb("comb", [P, B, TT, E])
        unit = sb("unit", [P, NB, TT])
        scale = sb("scale", [P, 2, NB, TT])
        tg = sb("tg", [P, 2])

        comb_in = ctx.enter_context(nc.semaphore("c_comb_in"))
        gate_in = ctx.enter_context(nc.semaphore("c_gate_in"))
        tg_ready = ctx.enter_context(nc.semaphore("c_tg_ready"))
        x_in = [ctx.enter_context(nc.semaphore(f"c_x_in{b}")) for b in range(NB)]
        acc_in = [ctx.enter_context(nc.semaphore(f"c_acc_in{b}")) for b in range(NB)]
        stored = [ctx.enter_context(nc.semaphore(f"c_stored{b}")) for b in range(NB)]
        raw_in = count("raw_in", 3 * 16)
        w_main = count("w_main", 1)
        w_rest = count("w_rest", 1, 1)
        scale_ready = count("scale_ready", 1)
        gate_sum = count("gate_sum", NB)
        up_sum = count("up_sum", NB)
        unit_ready = ctx.enter_context(nc.semaphore("c_unit_ready"))
        silu_done = count("silu_done", NB)
        hidden_done = count("hidden_done", NB)
        h_main = count("h_main", NB)
        h_rest = count("h_rest", NB)
        down_sum = count("down_sum", NB * TT)
        added = count("added", NB * TT)

        x_src = xt_dram
        acc_src = base_dram.rearrange("b (t p) c -> b p t c", p=P)
        out_dst = out.rearrange("b (t p) c -> b p t c", p=P)
        G0, U0, D0 = 0, KC * I, 2 * KC * I

        def gate_up(s, part, up, k, j):
            return weights[:, s, part, (U0 if up else G0) + k * I + j * P:(U0 if up else G0) + k * I + (j + 1) * P]

        def down(s, part, j):
            return weights[:, s, part, D0 + j * C:D0 + (j + 1) * C]

        block = ctx.enter_context(nc.Block())

        @block.sync
        def _(sp):
            def load_weights(step, g, u, d):
                wait_apart(sp, w_rest.sem, w_rest.at(step, 0), w_rest.sem)
                for w, at, n in ((g, G0, KC), (u, U0, KC), (d, D0, IC)):
                    size = n * (I if n == KC else C)
                    sp.dma_start(raw[:, at:at + size].rearrange("p (k n) -> p k n", k=n),
                                 w.rearrange("(k p) n -> p k n", p=P)).then_inc(raw_in.sem, 16)

            def load_batches(half):
                for b in range(NB):
                    if half:
                        sp.wait_ge(up_sum.sem, NB * E + b + 1)
                    sp.dma_start(xT[:, b].bitcast(F32), x_src[half * NB + b]).then_inc(x_in[b], 16)
                    if half:
                        sp.wait_ge(added.sem, TT * (NB * E + b + 1))
                        sp.dma_start(out_dst[b], acc[:, b]).then_inc(stored[b], 16)
                        sp.wait_ge(stored[b], 16)
                    sp.dma_start(acc[:, b], acc_src[half * NB + b]).then_inc(acc_in[b], 16)

            load_weights(0, s_gate[0], s_up[0], s_down[0])
            load_batches(0)
            sp.dma_start(comb[:], comb_dram.rearrange("b p t e -> p b t e")).then_inc(comb_in, 16)
            with sp.Fori(0, E) as e:
                load_weights(e + 1, w_gate[e], w_up[e], w_down[e])
            load_weights(E + 1, w_gate[0], w_up[0], w_down[0])
            load_batches(1)
            with sp.Fori(1, E) as e:
                load_weights(e + E + 1, w_gate[e], w_up[e], w_down[e])
            load_weights(STEPS - 1, s_gate[0], s_up[0], s_down[0])
            for b in range(NB):
                sp.wait_ge(added.sem, TT * (NB * (STEPS - 1) + b + 1))
                sp.dma_start(out_dst[NB + b], acc[:, b]).then_inc(stored[b], 16)
            for b in range(NB):
                sp.wait_ge(stored[b], 32)

        def order(eng, step):
            step(0, 0, 0, None)
            for half, first in ((0, 1), (1, E + 1)):
                with eng.Fori(0, E // 2) as e:
                    step(2 * e + first, 1, half, 2 * e)
                    step(2 * e + (first + 1), 0, half, 2 * e + 1)
            step(STEPS - 1, 1, 1, None)

        def is_first(half, e):
            return half == 0 and e is None

        def is_last(half, e):
            return half == 1 and e is None

        @block.gpsimd
        def _(pool):
            pool.dma_start(tg[:, 0:1], gate.partition_broadcast(P)).then_inc(gate_in, 16)
            pool.sem_inc(w_rest.sem, 1)

            def step(n, s, half, e):
                for b in range(NB):
                    pool.wait_ge(h_main.sem, h_main.at(n, b + 1))
                    nc.gpsimd.tensor_tensor(hT[:, b % 2, 1], hidden[:], hT[:, b % 2, 0].bitcast(F32),
                                            ALU.subtract).then_inc(h_rest.sem, 1)

            order(pool, step)

        @block.scalar
        def _(act):
            act.wait_ge(gate_in, 16)
            nc.scalar.activation(tg[:, 1:2], tg[:, 0:1], ACT.Tanh).then_inc(tg_ready, 1)

            def split(n, s):
                act.wait_ge(raw_in.sem, raw_in.at(n, 48))
                nc.scalar.activation(weights[:, s, 0], raw[:], ACT.Copy).then_inc(w_main.sem, 1)

            def step(n, s, half, e):
                for b in range(NB):
                    act.wait_ge(gate_sum.sem, gate_sum.at(n, b + 1))
                    nc.scalar.activation(silu[:], banks[:, 0:IC, :], ACT.Silu).then_inc(silu_done.sem, 1)
                    act.wait_ge(hidden_done.sem, hidden_done.at(n, b + 1))
                    nc.scalar.activation(hT[:, b % 2, 0], hidden[:], ACT.Copy).then_inc(h_main.sem, 1)
                    if b == 1 and not is_last(half, e):
                        split(n + 1, 1 - s)

            split(0, 0)
            order(act, step)

        @block.vector
        def _(dve):
            nc.vector.memset(unit[:], 1.0).then_inc(unit_ready, 1)
            dve.wait_ge(unit_ready, 1)
            dve.wait_ge(comb_in, 16)
            dve.wait_ge(tg_ready, 1)

            def split(n, s):
                dve.wait_ge(w_main.sem, w_main.at(n, 1))
                nc.vector.tensor_tensor(weights[:, s, 1], raw[:], weights[:, s, 0].bitcast(F32),
                                        ALU.subtract).then_inc(w_rest.sem, 1)

            def add(n, b, s):
                for t in range(TT):
                    dve.wait_ge(down_sum.sem, down_sum.at(n, b * TT + t + 1))
                    nc.vector.scalar_tensor_tensor(out=acc[:, b, t], in0=banks[:, 4 + t, :],
                                                   scalar=scale[:, s, b, t:t + 1], in1=acc[:, b, t],
                                                   op0=ALU.mult, op1=ALU.add).then_inc(added.sem, 1)

            def step(n, s, half, e):
                if e is None:
                    nc.vector.tensor_scalar(scale[:, s], unit[:], tg[:, 1:2], None, ALU.mult
                                            ).then_inc(scale_ready.sem, 1)
                else:
                    nc.vector.tensor_copy(scale[:, s], comb[:, half * NB:(half + 1) * NB, :, e]
                                          ).then_inc(scale_ready.sem, 1)
                for b in range(NB):
                    dve.wait_ge(up_sum.sem, up_sum.at(n, b + 1))
                    dve.wait_ge(silu_done.sem, silu_done.at(n, b + 1))
                    if b or not is_first(half, e):
                        dve.wait_ge(h_rest.sem, h_rest.at(n, b))
                    nc.vector.tensor_tensor(hidden[:], banks[:, IC:2 * IC, :], silu[:], ALU.mult
                                            ).then_inc(hidden_done.sem, 1)
                    if b == 0:
                        dve.wait_ge(scale_ready.sem, scale_ready.at(n, 1))
                        if not is_first(half, e):
                            if s == 0:
                                dve.wait_ge(acc_in[NB - 1], 16 * (half + 1))
                            add(n - 1, NB - 1, 1 - s)
                    else:
                        dve.wait_ge(acc_in[b - 1], 16 * (half + 1))
                        add(n, b - 1, s)
                    if b == 1 and not is_last(half, e):
                        split(n + 1, 1 - s)

            split(0, 0)
            order(dve, step)
            add(STEPS - 1, NB - 1, 1)

        @block.tensor
        def _(pe):
            def up(n, b, s, half, first):
                pe.wait_ge(x_in[b], 16 * (half + 1))
                if not first:
                    pe.wait_ge(hidden_done.sem, hidden_done.at(n, b))
                for is_up, done in ((False, gate_sum), (True, up_sum)):
                    for j in range(IC):
                        last = split_sum(pe, banks[:, IC * is_up + j, :],
                                         lambda a, k: gate_up(s, a, is_up, k, j), lambda a, k: xT[:, b, a, k, :],
                                         range(KC))
                    last.then_inc(done.sem, 1)

            def down_product(n, b, s, first=False):
                pe.wait_ge(h_rest.sem, h_rest.at(n, b + 1))
                for t in range(TT):
                    if not first:
                        pe.wait_ge(added.sem, added.at(n, (b - 1) * TT + t + 1))
                    split_sum(pe, banks[:, 4 + t, :], lambda a, j: hT[:, b % 2, a, j, t * P:(t + 1) * P],
                              lambda a, j: down(s, a, j), range(IC)).then_inc(down_sum.sem, 1)

            def step(n, s, half, e):
                pe.wait_ge(w_rest.sem, w_rest.at(n, 1))
                for b in range(NB):
                    up(n, b, s, half, b == 0 and is_first(half, e))
                    if b:
                        down_product(n, b - 1, s, b == 1 and is_first(half, e))
                    elif not is_first(half, e):
                        down_product(n - 1, NB - 1, 1 - s)

            order(pe, step)
            down_product(STEPS - 1, NB - 1, 1)


def program(nc, x, ctx, g_xattn, g_ffn, kv, q, proj, b_proj, w1, wq, kva, kvb, wo, w2, w_gate, e_bias,
            wg, wu, wd, swg, swu, swd, angles, out):
    def dram(name, shape):
        return nc.dram_tensor(name, shape, F32, kind="Internal").ap()

    x1 = dram("x1", (B, T, C))
    base = dram("base", (B, T, C))
    xt = dram("xt", (B, P, 2, KC, T))
    comb = dram("comb", (B, P, TT, w_gate.shape[1]))
    with nc.psum_tensor("banks", [P, 8, 512], F32) as banks:
        bank = [banks[:, n, :] for n in range(8)]
        cross_attention(nc, bank, x, ctx, kv, q, proj, b_proj, g_xattn, x1)
        self_attention_and_router(nc, bank, x1, w1, wq, kva, kvb, wo, w2, w_gate, e_bias, g_ffn, angles,
                                  base, xt, comb)
        experts(nc, banks, base, xt, comb, wg, wu, wd, swg, swu, swd, g_ffn, out)


def q_columns():
    D, J = 2 * HD, HD // 2
    plain = [(g * HG + h) * D + d for g in range(G) for d in range(HD) for h in range(HG)]
    rotated = [((2 * n + s) * HG + h) * D + HD + 2 * j + e
               for n in range(G // 2) for e in range(2) for s in range(2) for j in range(J) for h in range(HG)]
    return plain + rotated


def kva_columns(latent):
    return list(range(latent)) + [latent + 2 * j + e for e in range(2) for j in range(HD // 2)]


def rope_angles():
    import numpy as np
    f = np.float32
    freqs = (f(1.0) / f(100000.0) ** (np.arange(0, HD, 2, dtype=f) / f(HD))).astype(f)
    ang = np.outer(freqs, np.arange(T, dtype=f)).astype(f)
    t = np.repeat(np.stack([np.cos(ang), np.sin(ang)]).astype(f), HG, axis=1)
    return np.ascontiguousarray(np.concatenate([t, t], axis=1))


def kernel(**inputs):
    import numpy as np
    import concourse.bacc as bacc
    from concourse.bass_utils import run_bass_kernel_spmd as run

    a, f = "L0_xattn_", "L0_ffn_"
    a_in = {k: np.asarray(v) for k, v in inputs.items()}
    by_partition = lambda w: w.reshape(KC, P).T
    laid_out = [
        ("x", a_in["x"]), ("ctx", a_in["ctx_1024"]), ("g_xattn", a_in["g_xattn"]), ("g_ffn", a_in["g_ffn"]),
        ("W_kv", a_in[a + "W_kv"]), ("W_q", a_in[a + "W_q"]), ("W_proj", a_in[a + "W_proj"]),
        ("b_proj", a_in[a + "b_proj"]), ("w_ln1", by_partition(a_in[f + "w_ln1"])),
        ("Wq", a_in[f + "Wq"][:, q_columns()]), ("Wkva", a_in[f + "Wkva"][:, kva_columns(a_in[f + "Wkvb"].shape[0])]),
        ("Wkvb", a_in[f + "Wkvb"]), ("Wo", a_in[f + "Wo"]), ("w_ln2", by_partition(a_in[f + "w_ln2"])),
        ("Wgate", a_in[f + "Wgate"]), ("expert_bias", a_in[f + "expert_bias"]),
        ("Wg", a_in[f + "Wg"]), ("Wu", a_in[f + "Wu"]), ("Wd", a_in[f + "Wd"]),
        ("sWg", a_in[f + "sWg"]), ("sWu", a_in[f + "sWu"]), ("sWd", a_in[f + "sWd"]),
        ("angles", rope_angles()),
    ]
    nc = bacc.Bacc("TRN2", target_bir_lowering=False, num_devices=1)
    arrays, args = {}, []
    for name, array in laid_out:
        array = np.ascontiguousarray(array)
        arrays[f"in_{name}"] = array
        args.append(nc.dram_tensor(f"in_{name}", array.shape, mybir.dt.from_np(array.dtype),
                                   kind="ExternalInput").ap())
    out = nc.dram_tensor("out_0", (B, T, C), F32, kind="ExternalOutput").ap()
    program(nc, *args, out)
    r = run(nc, [arrays], core_ids=[0])
    return r.results[0]["out_0"]
```

```python
import math
from contextlib import ExitStack

import concourse.bass as bass
from concourse import mybir

ALU = mybir.AluOpType
ACT = mybir.ActivationFunctionType
AX_X = mybir.AxisListType.X
F32 = mybir.dt.float32
F32R = mybir.dt.float32r
U32 = mybir.dt.uint32

P = 128
B, T, C = 8, 512, 512
KC = C // P
TT = T // P
H = 16
HD = 32
HG = P // HD
G = H // HG
EPS = 1e-5
TERMS = ((0, 0), (1, 0), (0, 1))


class Count:

    def __init__(self, ctx, nc, name, per_turn, credit=0):
        self.sem = ctx.enter_context(nc.semaphore(name))
        self.name, self.per_turn, self.credit, self.made = name, per_turn, credit, 0

    def at(self, turn, n):
        return turn * self.per_turn + (n + self.credit)


def split_sum(pe, out, stationary, moving, chunks):
    n, last = 0, None
    for k in chunks:
        for a, b in TERMS:
            last = pe.matmul(out, stationary(a, k), moving(b, k), start=(n == 0),
                             stop=(n == 3 * len(chunks) - 1))
            n += 1
    return last


def wait_apart(eng, sem, value, passed):
    eng.wait_ge(passed, 1)
    eng.wait_ge(sem, value)


def wait_by_memset(nc, sem, value, scratch):
    nc.vector.wait_ge(sem, value)
    nc.vector.memset(scratch, 0.0)


def cross_attention(nc, bank, x, ctx_in, w_kv, w_q, w_proj, b_proj, gate, x1_dram):
    SCALE = HD ** -0.5
    PIECES = 3
    with ExitStack() as ctx:
        def sb(name, shape, dt=F32):
            return ctx.enter_context(nc.sbuf_tensor("a_" + name, shape, dt))

        def sem(name):
            return ctx.enter_context(nc.semaphore("a_" + name))

        def count(name, per_turn, credit=0):
            return Count(ctx, nc, "a_" + name, per_turn, credit)

        wq = sb("wq", [P, 2, KC, C], F32R)
        wk = sb("wk", [P, 2, KC, C], F32R)
        wv = sb("wv", [P, 2, KC, C], F32R)
        wp = sb("wp", [P, 2, KC, C], F32R)
        ident = sb("ident", [P, P])
        ones = sb("ones", [P, HD])
        bias = sb("bias", [P, C])
        tg = sb("tg", [P, 2])
        x_tok = sb("x_tok", [P, TT, C])
        ctx_tok = sb("ctx_tok", [P, TT, C])
        res = sb("res", [P, TT, C])
        ctxT = sb("ctxT", [P, 2, KC, T], F32R)
        xT = sb("xT", [P, 2, KC, T], F32R)
        oT = sb("oT", [P, 2, G, T], F32R)
        qk = sb("qk", [P, 2, 2, T], F32R)
        q_stack = sb("q_stack", [97, 2, HG, T], F32R)
        k_stack = sb("k_stack", [97, 2, HG, T], F32R)
        v = sb("v", [P, TT, C])
        prob = sb("prob", [P, 2, HG, T])
        xn = prob[:, 0]
        o_norm = sb("o_norm", [P, T])
        neg_max = sb("neg_max", [P, 2, HG * TT])
        max_row = sb("max_row", [HG * TT, 2, P], F32R)
        waited = sb("waited", [P, 1])
        st6 = sb("st6", [P, TT, 6])
        mv = sb("mv", [P, TT, 2])
        veps = sb("veps", [P, TT])
        mhalf = sb("mhalf", [P, TT])
        rstd = sb("rstd", [P, TT])

        w_in = [sem(f"w_in{n}") for n in range(4)]
        small_in = sem("small_in")
        w_main = sem("w_main")
        w_rest = sem("w_rest")
        const_ready = sem("const_ready")
        fill_ready = sem("fill_ready")
        tg_ready = sem("tg_ready")
        bias_ready = sem("bias_ready")
        wp_main = sem("wp_main")
        wp_rest = sem("wp_rest")

        x_in = count("x_in", 16)
        ctx_load = count("ctx_load", 16)
        res_ready = count("res_ready", TT)
        res_stored = count("res_stored", 16, 16)
        veps_ready = count("veps_ready", 1)
        rstd_ready = count("rstd_ready", 1)
        xn_ready = count("xn_ready", TT)
        turned = count("turned", 2 * KC)
        turned_main = count("turned_main", 2 * KC)
        turned_rest = count("turned_rest", 2 * KC)
        v_sum = count("v_sum", TT)
        v_ready = count("v_ready", TT)
        qk_sum = count("qk_sum", 2 * G)
        qk_main = count("qk_main", 2 * G)
        qk_rest = count("qk_rest", 2 * G)
        q_in = [count(f"q_in{s}", G // 2 * PIECES * 16) for s in range(2)]
        k_in = [count(f"k_in{s}", G // 2 * PIECES * 16) for s in range(2)]
        max_sum = count("max_sum", H * TT)
        max_done = count("max_done", H * TT)
        max_turned = count("max_turned", G)
        row_ready = count("row_ready", G)
        row_in = [count(f"row_in{s}", G // 2 * 16) for s in range(2)]
        score_sum = count("score_sum", H * TT)
        exp_done = count("exp_done", H * TT)
        pv_done = count("pv_done", G * TT)
        recip_done = count("recip_done", G)
        o_ready = count("o_ready", G)
        o_main = count("o_main", G)
        o_rest = count("o_rest", G)
        proj_sum = count("proj_sum", TT)
        x1_ready = count("x1_ready", TT, TT)
        dve_step = count("dve_step", TT + 1)

        w_src = [w_q.rearrange("(k p) n -> p k n", p=P),
                 w_kv[:, 0:C].rearrange("(k p) n -> p k n", p=P),
                 w_kv[:, C:2 * C].rearrange("(k p) n -> p k n", p=P),
                 w_proj.rearrange("(k p) n -> p k n", p=P)]
        w_dst = [wq, wk, wv, wp]
        w_raw = [v[:], prob[:, 1], res[:], prob[:, 0]]
        x_src = x.rearrange("b (t p) c -> b p t c", p=P)
        ctx_src = ctx_in.rearrange("b (t p) c -> b p t c", p=P)
        x1_dst = x1_dram.rearrange("b (t p) c -> b p t c", p=P)
        next_x, next_ctx = x_src[1:B], ctx_src[1:B]

        def columns(n, w, placed=False):
            order = "p (g d h) -> p g h d" if placed and n < 2 else "p (g h d) -> p g h d"
            return w.rearrange(order, h=HG, d=HD)

        def turns(eng, turn):
            with eng.Fori(0, B - 1) as i:
                turn(i, False)
            turn(B - 1, True)

        def qk_bank(g, w):
            return 5 - w + 2 * (g == 1)

        def pieces_in(counts, i, g):
            return counts[g % 2].sem, counts[g % 2].at(i, PIECES * 16 * (g // 2 + 1))

        TURN_BANK = (4, 5, 0, 1, 2, 3, 6, 7)
        MAXIMA_STEPS = ((2, 2, 2, 2, 2, 2, 1, 1, 1, 1), (0, 0, 0, 0, 3, 3, 3, 3, 2, 2))

        block = ctx.enter_context(nc.Block())

        @block.sync
        def _(sp):
            sp.dma_start(ctx_tok[:], ctx_src[0]).then_inc(ctx_load.sem, 16)
            sp.dma_start(x_tok[:], x_src[0]).then_inc(x_in.sem, 16)
            for n in range(4):
                if n == 3:
                    sp.wait_ge(turned.sem, turned.at(0, 2 * KC))
                sp.dma_start(w_raw[n], w_src[n]).then_inc(w_in[n], 16)

            def turn(i, last):
                def q_pieces(g):
                    if g < 2:
                        sp.wait_ge(qk_rest.sem, qk_rest.at(i, 2 * g + 1))
                    else:
                        sp.wait_ge(score_sum.sem, score_sum.at(i, (g - 1) * TT * HG))
                    for piece, part in enumerate((0, 0, 1)):
                        sp.dma_start(q_stack[HD * piece:HD * (piece + 1), g % 2, :, :].bitcast(F32),
                                     qk[:, 0, part, :].bitcast(F32)).then_inc(q_in[g % 2].sem, 16)

                def k_pieces(g):
                    sp.wait_ge(qk_rest.sem, qk_rest.at(i, 2 * g + 2))
                    for piece, part in enumerate((0, 1, 0)):
                        sp.dma_start(k_stack[HD * piece:HD * (piece + 1), g % 2, :, :].bitcast(F32),
                                     qk[:, 1, part, :].bitcast(F32)).then_inc(k_in[g % 2].sem, 16)

                def row(g):
                    sp.wait_ge(row_ready.sem, row_ready.at(i, g + 1))
                    sp.dma_start(q_stack[96:97, g % 2, :, :].bitcast(F32),
                                 max_row[:, g % 2, :].bitcast(F32)).then_inc(row_in[g % 2].sem, 16)

                for g in range(2):
                    q_pieces(g)
                    k_pieces(g)
                row(0)
                if not last:
                    sp.wait_ge(turned.sem, turned.at(i, 2 * KC))
                    sp.dma_start(ctx_tok[:], next_ctx[i]).then_inc(ctx_load.sem, 16)
                    sp.wait_ge(res_ready.sem, res_ready.at(i, TT))
                    sp.dma_start(x_tok[:], next_x[i]).then_inc(x_in.sem, 16)
                for g in range(2, G):
                    q_pieces(g)
                    row(g - 1)
                    k_pieces(g)
                row(G - 1)

            turns(sp, turn)

        @block.gpsimd
        def _(pool):
            pool.dma_start(tg[:, 0:1], gate.partition_broadcast(P)).then_inc(small_in, 16)
            pool.dma_start(bias[:], b_proj.partition_broadcast(P)).then_inc(small_in, 16)
            nc.gpsimd.memset(ident[:], 0.0).then_inc(const_ready, 1)
            pool.wait_ge(const_ready, 1)
            nc.gpsimd.affine_select(out=ident[:], in_=ident[:], compare_op=ALU.not_equal, fill=1.0, base=0,
                                    pattern=[[-1, P]], channel_multiplier=1).then_inc(const_ready, 1)
            pool.wait_ge(tg_ready, 1)
            pool.wait_ge(fill_ready, 1)

            def deviation(i):
                pool.wait_ge(veps_ready.sem, veps_ready.at(i, 1))
                nc.gpsimd.tensor_tensor(rstd[:], veps[:], mhalf[:], ALU.pow).then_inc(rstd_ready.sem, 1)

            deviation(0)
            nc.gpsimd.tensor_scalar(bias[:], bias[:], tg[:, 1:2], 1.0, ALU.mult, ALU.mult).then_inc(bias_ready, 1)
            pool.wait_ge(w_in[3], 16)
            nc.gpsimd.tensor_copy(wp[:, 0], w_raw[3]).then_inc(wp_main, 1)
            pool.wait_ge(wp_main, 1)
            nc.gpsimd.tensor_tensor(wp[:, 1], w_raw[3], wp[:, 0].bitcast(F32), ALU.subtract).then_inc(wp_rest, 1)
            pool.wait_ge(bias_ready, 1)
            pool.wait_ge(wp_rest, 1)
            pool.wait_ge(w_rest, 3)

            def turn(i, last):
                pool.wait_ge(x_in.sem, x_in.at(i, 16))
                pool.wait_ge(res_stored.sem, res_stored.at(i, 0))
                for t in range(TT):
                    nc.gpsimd.tensor_tensor(res[:, t], x_tok[:, t], bias[:], ALU.add).then_inc(res_ready.sem, 1)
                for g in range(G):
                    if g == G - 1 and not last:
                        deviation(i + 1)
                    pool.wait_ge(o_main.sem, o_main.at(i, g + 1))
                    nc.gpsimd.tensor_tensor(oT[:, 1, g, :], o_norm[:], oT[:, 0, g, :].bitcast(F32),
                                            ALU.subtract).then_inc(o_rest.sem, 1)

            turns(pool, turn)

        @block.scalar
        def _(act):
            act.sem_inc(res_stored.sem, 16)
            act.wait_ge(small_in, 32)
            nc.scalar.activation(tg[:, 1:2], tg[:, 0:1], ACT.Tanh).then_inc(tg_ready, 1)

            def turned_mains(i, chunks):
                for n in chunks:
                    act.wait_ge(turned.sem, turned.at(i, n + 1))
                    nc.scalar.activation((ctxT, xT)[n // KC][:, 0, n % KC, :], bank[TURN_BANK[n]],
                                         ACT.Copy).then_inc(turned_main.sem, 1)

            def weight_main(n):
                act.wait_ge(w_in[n], 16)
                for k in range(KC):
                    last = nc.scalar.activation(columns(n, w_dst[n][:, 0, k], True), columns(n, w_raw[n][:, k]),
                                                ACT.Copy)
                last.then_inc(w_main, 1)

            turned_mains(0, range(KC))
            turned_mains(0, range(KC, 2 * KC))
            for n in range(3):
                weight_main(n)
            act.wait_ge(w_rest, 3)

            def turn(i, last):
                def qk_main_of(g, w):
                    act.wait_ge(qk_sum.sem, qk_sum.at(i, 2 * g + w + 1))
                    if g:
                        act.wait_ge(*pieces_in((q_in, k_in)[w], i, g - 1))
                    nc.scalar.activation(qk[:, w, 0, :], bank[qk_bank(g, w)], ACT.Copy).then_inc(qk_main.sem, 1)

                def output_main(g):
                    act.wait_ge(o_ready.sem, o_ready.at(i, g + 1))
                    nc.scalar.activation(oT[:, 0, g, :], o_norm[:], ACT.Copy).then_inc(o_main.sem, 1)

                def v_copies(tiles):
                    for t in tiles:
                        act.wait_ge(v_sum.sem, v_sum.at(i, t + 1))
                        nc.scalar.activation(v[:, t, :], bank[4 + t % 2], ACT.Copy).then_inc(v_ready.sem, 1)

                qk_main_of(0, 0)
                qk_main_of(0, 1)
                v_copies((0,))
                qk_main_of(1, 0)
                qk_main_of(1, 1)
                v_copies((1, 2, 3))
                qk_main_of(2, 0)
                act.wait_ge(wp_rest, 1)
                for g in range(G):
                    if g == G - 1 and not last:
                        turned_mains(i + 1, (0, 1))
                    for k in range(TT):
                        for h in range(HG):
                            n = (g * TT + k) * HG + h
                            act.wait_ge(score_sum.sem, score_sum.at(i, n + 1))
                            if n >= 2 * HG:
                                act.wait_ge(pv_done.sem, pv_done.at(i, n // HG - 1))
                            nc.scalar.activation(prob[:, k % 2, h, :], bank[h], ACT.Exp,
                                                 scale=SCALE).then_inc(exp_done.sem, 1)
                        if k == 0 and g:
                            output_main(g - 1)
                        if k == 0 and 0 < g < G - 2:
                            qk_main_of(g + 2, 0)
                    if g + 2 < G:
                        qk_main_of(g + 2, 1)
                    if g == G - 1 and not last:
                        turned_mains(i + 1, range(2, KC + 2))
                output_main(G - 1)
                if not last:
                    turned_mains(i + 1, range(KC + 2, 2 * KC))
                act.wait_ge(x1_ready.sem, x1_ready.at(i, TT))
                act.dma_start(x1_dst[i], res[:]).then_inc(res_stored.sem, 16)

            turns(act, turn)
            act.wait_ge(res_stored.sem, res_stored.at(B, 0))

        @block.vector
        def _(dve):
            nc.vector.memset(mhalf[:], -0.5).then_inc(fill_ready, 1)
            nc.vector.memset(ones[:], 1.0).then_inc(fill_ready, 1)
            nc.vector.memset(k_stack[96:97, :, :, :].bitcast(F32), 1.0).then_inc(fill_ready, 1)
            dve.sem_inc(x1_ready.sem, TT)

            def statistics(i):
                dve.wait_ge(x_in.sem, x_in.at(i, 16))
                for t in range(TT):
                    nc.vector.bn_stats(st6[:, t], x_tok[:, t]).then_inc(dve_step.sem, 1)
                wait_by_memset(nc, dve_step.sem, dve_step.at(i, TT), waited[:])
                for t in range(TT):
                    last = nc.vector.bn_aggr(mv[:, t], st6[:, t])
                last.then_inc(dve_step.sem, 1)
                dve.wait_ge(dve_step.sem, dve_step.at(i, TT + 1))
                nc.vector.tensor_scalar(veps[:], mv[:, :, 1], EPS, None, ALU.add).then_inc(veps_ready.sem, 1)

            def normalise(i):
                dve.wait_ge(rstd_ready.sem, rstd_ready.at(i, 1))
                for t in range(TT):
                    nc.vector.tensor_scalar(xn[:, t], x_tok[:, t], mv[:, t, 0:1], rstd[:, t:t + 1],
                                            ALU.subtract, ALU.mult).then_inc(xn_ready.sem, 1)

            def turned_rests(i, chunks):
                for n in chunks:
                    dst = (ctxT, xT)[n // KC][:, :, n % KC, :]
                    dve.wait_ge(turned_main.sem, turned_main.at(i, n + 1))
                    nc.vector.tensor_tensor(dst[:, 1], bank[TURN_BANK[n]], dst[:, 0].bitcast(F32),
                                            ALU.subtract).then_inc(turned_rest.sem, 1)

            def weight_rest(n):
                dve.wait_ge(w_main, n + 1)
                for k in range(KC):
                    last = nc.vector.tensor_tensor(columns(n, w_dst[n][:, 1, k], True),
                                                   columns(n, w_raw[n][:, k]),
                                                   columns(n, w_dst[n][:, 0, k].bitcast(F32), True), ALU.subtract)
                last.then_inc(w_rest, 1)

            turned_rests(0, range(KC))
            statistics(0)
            normalise(0)
            turned_rests(0, range(KC, 2 * KC))
            for n in range(3):
                weight_rest(n)

            def turn(i, last):
                def qk_rest_of(g, w):
                    dve.wait_ge(qk_main.sem, qk_main.at(i, 2 * g + w + 1))
                    nc.vector.tensor_tensor(qk[:, w, 1, :], bank[qk_bank(g, w)], qk[:, w, 0, :].bitcast(F32),
                                            ALU.subtract).then_inc(qk_rest.sem, 1)

                def maxima(g, t):
                    for h in range(HG):
                        n = (g * TT + t) * HG + h
                        dve.wait_ge(max_sum.sem, max_sum.at(i, n + 1))
                        b = n % 4 if g == 0 else 4 + n % 2
                        nc.vector.tensor_reduce(neg_max[:, g % 2, h * TT + t:h * TT + t + 1], bank[b],
                                                AX_X, ALU.max, negate=True).then_inc(max_done.sem, 1)

                def rows(g):
                    dve.wait_ge(max_turned.sem, max_turned.at(i, g + 1))
                    nc.vector.tensor_copy(max_row[:, g % 2, :], bank[0][0:HG * TT, 0:P]).then_inc(row_ready.sem, 1)

                qk_rest_of(0, 0)
                qk_rest_of(0, 1)
                for t in range(TT):
                    maxima(0, t)
                    if t == 0:
                        qk_rest_of(1, 0)
                        qk_rest_of(1, 1)
                rows(0)
                for g in range(G):
                    if g + 2 < G:
                        qk_rest_of(g + 2, 0)
                    if g + 1 < G:
                        for t in range(TT):
                            maxima(g + 1, t)
                        rows(g + 1)
                    elif not last:
                        turned_rests(i + 1, (0, 1))
                        statistics(i + 1)
                        dve.wait_ge(pv_done.sem, pv_done.at(i, TT * G - 1))
                        normalise(i + 1)
                    dve.wait_ge(pv_done.sem, pv_done.at(i, TT * (g + 1)))
                    if g:
                        dve.wait_ge(o_rest.sem, o_rest.at(i, g))
                    nc.vector.reciprocal(o_norm[:], bank[7]).then_inc(recip_done.sem, 1)
                    if g + 2 < G:
                        qk_rest_of(g + 2, 1)
                    dve.wait_ge(recip_done.sem, recip_done.at(i, g + 1))
                    nc.vector.tensor_tensor(o_norm[:], bank[6], o_norm[:], ALU.mult).then_inc(o_ready.sem, 1)
                if not last:
                    turned_rests(i + 1, range(2, 2 * KC))
                dve.wait_ge(res_ready.sem, res_ready.at(i, TT))
                for t in range(TT):
                    dve.wait_ge(proj_sum.sem, proj_sum.at(i, t + 1))
                    nc.vector.scalar_tensor_tensor(out=res[:, t], in0=bank[t], scalar=tg[:, 1:2], in1=res[:, t],
                                                   op0=ALU.mult, op1=ALU.add).then_inc(x1_ready.sem, 1)

            turns(dve, turn)

        @block.tensor
        def _(pe):
            pe.wait_ge(const_ready, 2)
            pe.wait_ge(fill_ready, 3)

            def turn_in(i, chunks):
                for n in chunks:
                    for t in range(TT):
                        if n < KC:
                            pe.wait_ge(ctx_load.sem, ctx_load.at(i, 16))
                        else:
                            pe.wait_ge(xn_ready.sem, xn_ready.at(i, t + 1))
                        last = pe.transpose(bank[TURN_BANK[n]][:, t * P:(t + 1) * P],
                                            (ctx_tok, xn)[n // KC][:, t, (n % KC) * P:(n % KC + 1) * P], ident[:])
                    last.then_inc(turned.sem, 1)

            turn_in(0, range(2 * KC))

            def turn(i, last):
                def project(g, w):
                    weight, src = ((wq, xT), (wk, ctxT))[w]
                    split_sum(pe, bank[qk_bank(g, w)], lambda a, k: weight[:, a, k, g * P:(g + 1) * P],
                              lambda a, k: src[:, a, k, :], range(KC)).then_inc(qk_sum.sem, 1)

                def max_score(g, n):
                    t, h = n // HG, n % HG
                    n += g * TT * HG
                    b = n % 4 if g == 0 else 4 + n % 2
                    ring = 4 if g == 0 else 2
                    if n >= ring:
                        pe.wait_ge(max_done.sem, max_done.at(i, n + 1 - ring))
                    pe.matmul(bank[b], q_stack[0:96, g % 2, h, t * P:(t + 1) * P],
                              k_stack[0:96, g % 2, h, :], start=True, stop=True).then_inc(max_sum.sem, 1)

                def turn_max(g):
                    pe.wait_ge(max_done.sem, max_done.at(i, (g + 1) * TT * HG))
                    if g:
                        pe.wait_ge(exp_done.sem, exp_done.at(i, g * TT * HG))
                    pe.transpose(bank[0][0:HG * TT, 0:P], neg_max[:, g % 2, :], ident[:]).then_inc(max_turned.sem, 1)

                def scores(g, k, h):
                    n = (g * TT + k) * HG + h
                    if n >= HG:
                        pe.wait_ge(exp_done.sem, exp_done.at(i, n + 1 - HG))
                    pe.matmul(bank[h], k_stack[:, g % 2, h, k * P:(k + 1) * P], q_stack[:, g % 2, h, :],
                              start=True, stop=True).then_inc(score_sum.sem, 1)

                def weigh(g, k, sums):
                    if not sums:
                        pe.wait_ge(exp_done.sem, exp_done.at(i, (g * TT + k + 1) * HG))
                        if k == 0 and g:
                            pe.wait_ge(o_ready.sem, o_ready.at(i, g))
                    for h in range(HG):
                        out = bank[7 if sums else 6][HD * h:HD * (h + 1), :]
                        c = g * P + h * HD
                        last = pe.matmul(out, ones[:] if sums else v[:, k, c:c + HD], prob[:, k % 2, h, :],
                                         start=(k == 0), stop=(k == TT - 1))
                    if sums:
                        last.then_inc(pv_done.sem, 1)

                def values(t):
                    if t < 2:
                        pe.wait_ge(qk_rest.sem, qk_rest.at(i, 2 - t))
                    else:
                        pe.wait_ge(v_ready.sem, v_ready.at(i, t - 1))
                    split_sum(pe, bank[4 + t % 2], lambda a, k: ctxT[:, a, k, t * P:(t + 1) * P],
                              lambda a, k: wv[:, a, k, :], range(KC)).then_inc(v_sum.sem, 1)

                pe.wait_ge(turned_rest.sem, turned_rest.at(i, 2 * KC))
                pe.wait_ge(w_rest, 2)
                for g in range(2):
                    for w in range(2):
                        project(g, w)
                pe.wait_ge(w_rest, 3)
                values(0)
                pe.wait_ge(x1_ready.sem, x1_ready.at(i, 0))
                pe.wait_ge(*pieces_in(q_in, i, 0))
                pe.wait_ge(*pieces_in(k_in, i, 0))
                for t in range(TT):
                    for h in range(HG):
                        max_score(0, t * HG + h)
                    if t + 1 < TT:
                        values(t + 1)
                turn_max(0)
                pe.wait_ge(v_ready.sem, v_ready.at(i, TT))
                project(2, 0)
                pe.wait_ge(qk_rest.sem, qk_rest.at(i, 4))
                for g in range(G):
                    pe.wait_ge(row_in[g % 2].sem, row_in[g % 2].at(i, (g // 2 + 1) * 16))
                    n = 0
                    for step, maxima in enumerate(MAXIMA_STEPS[min(g, 1)]):
                        k, half = step // 2, step % 2
                        if step == 2 and 0 < g < G - 2:
                            project(g + 2, 0)
                        if n == 0 and maxima and g + 1 < G:
                            pe.wait_ge(*pieces_in(q_in, i, g + 1))
                            pe.wait_ge(*pieces_in(k_in, i, g + 1))
                            if g + 2 < G:
                                pe.wait_ge(qk_rest.sem, qk_rest.at(i, 2 * g + 5))
                        for j in range(max(2, maxima)):
                            if k < TT and j < 2:
                                scores(g, k, 2 * half + j)
                            if j < maxima and g + 1 < G:
                                max_score(g + 1, n)
                                n += 1
                        if k:
                            weigh(g, k - 1, half == 1)
                    if g + 1 < G:
                        turn_max(g + 1)
                    if g + 2 < G:
                        project(g + 2, 1)
                    elif g + 1 < G and not last:
                        turn_in(i + 1, (0, 1))
                if not last:
                    turn_in(i + 1, range(2, KC + 2))
                    pe.wait_ge(o_ready.sem, o_ready.at(i, G))
                    turn_in(i + 1, range(KC + 2, 2 * KC))
                pe.wait_ge(wp_rest, 1)
                pe.wait_ge(o_rest.sem, o_rest.at(i, G))
                for t in range(TT):
                    if not last:
                        pe.wait_ge(turned_rest.sem, turned_rest.at(i + 1, t + 3))
                    split_sum(pe, bank[t], lambda a, k: oT[:, a, k, t * P:(t + 1) * P],
                              lambda a, k: wp[:, a, k, :], range(KC)).then_inc(proj_sum.sem, 1)

            turns(pe, turn)


def self_attention_and_router(nc, bank, x1_dram, w_ln1, w_q, w_kva, w_kvb, w_o, w_ln2, w_gate, e_bias, gate,
                              angles, base_dram, xt_dram, comb_dram):
    D = 2 * HD
    SCALE = D ** -0.5
    R = w_kvb.shape[0]
    E = w_gate.shape[1]
    J = HD // 2
    BIG = -1e30
    PIECES = 3
    ROPE_BANKS = ((7, 4), (1, 2))
    QK_BANK = ((5, 6), (5, 6), (3, 4), (5, 4))
    TURN_BANK = (4, 5, 2, 3)
    MAXIMA_STEPS = ((0, 0, 2, 2, 2, 2, 2, 2, 2, 2), (0, 0, 0, 0, 3, 3, 3, 3, 2, 2))

    with ExitStack() as ctx:
        def sb(name, shape, dt=F32):
            return ctx.enter_context(nc.sbuf_tensor("b_" + name, shape, dt))

        def sem(name):
            return ctx.enter_context(nc.semaphore("b_" + name))

        def count(name, per_turn, credit=0):
            return Count(ctx, nc, "b_" + name, per_turn, credit)

        wq = sb("wq", [P, 2, KC, H * D], F32R)
        wkva = sb("wkva", [P, 2, KC, P], F32R)
        wkvb_k = sb("wkvb_k", [R, 2, C], F32R)
        wkvb_v = sb("wkvb_v", [R, 2, C], F32R)
        wo = sb("wo", [P, 2, G, C], F32R)
        wgate = sb("wgate", [P, 2, KC, E], F32R)
        gate_raw = sb("gate_raw", [P, KC, E])
        w1 = sb("w1", [P, KC])
        w2 = sb("w2", [P, KC])
        ebias = sb("ebias", [P, E])
        expert = sb("expert", [P, E])
        ident = sb("ident", [P, P])
        ident_r = sb("ident_r", [P, P], F32R)
        mask_q = sb("mask_q", [P, P], F32R)
        mask_k = sb("mask_k", [P, P], F32R)
        ones = sb("ones", [P, HD])
        tg = sb("tg", [P, 2])
        cs = sb("cs", [P, 2, T])
        x_tok = sb("x_tok", [P, TT, C])
        hT = sb("hT", [P, 2, KC, T], F32R)
        oT = sb("oT", [P, 2, G, T], F32R)
        qk = sb("qk", [P, 2, 2, T], F32R)
        rope = sb("rope", [P, 2, 2, T], F32R)
        tmp = sb("tmp", [P, T])
        o_norm = sb("o_norm", [P, T])
        lat = sb("lat", [R, 2, T], F32R)
        csk = x_tok[96:96 + J, 0:2, :]
        krope = x_tok[96:96 + J, 2:4, :]
        q_stack = sb("q_stack", [97, 2, HG, T], F32R)
        k_stack = sb("k_stack", [97, 2, HG, T], F32R)
        qr_stack = sb("qr_stack", [96, 2, HG, T], F32R)
        kr_stack = sb("kr_stack", [96, T], F32R)
        v = sb("v", [P, TT, C])
        prob = sb("prob", [P, 2, HG, T])
        xn = prob[:, 0]
        krope_work = prob[96:96 + J, 0, 2:4, :]
        rope_k = [[prob[96:96 + J, 0, n, :].bitcast(F32R) for n in range(2)],
                  [krope[:, n, :].bitcast(F32R) for n in range(2)]]
        x_back = prob[:, 1]
        y2 = v
        yT = oT
        neg_max = sb("neg_max", [P, 2, HG * TT])
        max_row = sb("max_row", [HG * TT, 2, P], F32R)
        waited = sb("waited", [P, 1])
        st6 = sb("st6", [P, TT, 6])
        mv = sb("mv", [P, TT, 2])
        kept = sb("kept", [P, 2, TT])
        stat = sb("stat", [P, 6, TT])
        mhalf = sb("mhalf", [P, TT])
        ssq = sb("ssq", [P, 3, TT])
        logit_row = prob[0:E, 0, 0, :]
        logit = sb("logit", [P, TT, E])
        top = sb("top", [P, TT, 8])
        index = sb("index", [P, TT, 8], U32)
        index_f = sb("index_f", [P, TT, 8])
        pick = sb("pick", [P, 5, TT])
        one_hot = sb("one_hot", [P, 2, TT, E])
        comb = sb("comb", [P, TT, E])

        w_in = [sem(f"w_in{n}") for n in range(4)]
        w_main = sem("w_main")
        w_rest = sem("w_rest")
        small_in = sem("small_in")
        angles_in = sem("angles_in")
        kva_zero = sem("kva_zero")
        fill_ready = sem("fill_ready")
        mask_step = sem("mask_step")
        const_ready = sem("const_ready")
        tg_ready = sem("tg_ready")

        x_in = count("x_in", 16)
        stat_step = count("stat_step", TT + 4)
        var_ready = count("var_ready", 1)
        rstd_ready = count("rstd_ready", 1)
        ms_ready = count("ms_ready", 1)
        rms_ready = count("rms_ready", 1)
        h_ready = count("h_ready", TT)
        kept_ready = count("kept_ready", 1)
        turned = count("turned", KC)
        turned_main = count("turned_main", KC)
        turned_rest = count("turned_rest", KC)
        y_turned = count("y_turned", KC)
        y_main = count("y_main", KC)
        y_rest = count("y_rest", KC)
        lat_sum = count("lat_sum", 1)
        lat_main = count("lat_main", 3)
        lat_rest = count("lat_rest", 1)
        krope_step = count("krope_step", 6)
        krope_main = count("krope_main", 2)
        krope_rest = count("krope_rest", 2)
        csk_in = count("csk_in", 2 * 16)
        krope_in = count("krope_in", 2 * PIECES * 16)
        v_sum = count("v_sum", TT)
        v_ready = count("v_ready", TT)
        qk_sum = count("qk_sum", 2 * G)
        qk_main = count("qk_main", 2 * G)
        qk_rest = count("qk_rest", 2 * G)
        rope_sum = count("rope_sum", 4)
        rope_step = count("rope_step", 2 * 6)
        rope_main = count("rope_main", 4)
        rope_rest = count("rope_rest", 4)
        q_in = [count(f"q_in{s}", G // 2 * PIECES * 16) for s in range(2)]
        k_in = [count(f"k_in{s}", G // 2 * PIECES * 16) for s in range(2)]
        rotated_in = [count(f"rotated_in{s}", G // 2 * 2 * PIECES * 16) for s in range(2)]
        x_again = count("x_again", 16)
        max_sum = count("max_sum", H * TT)
        max_done = count("max_done", H * TT)
        max_turned = count("max_turned", G)
        row_ready = count("row_ready", G)
        row_in = [count(f"row_in{s}", G // 2 * 16) for s in range(2)]
        score_sum = count("score_sum", H * TT)
        exp_done = count("exp_done", H * TT)
        pv_done = count("pv_done", G * TT)
        recip_done = count("recip_done", G)
        o_ready = count("o_ready", G)
        o_main = count("o_main", G)
        o_rest = count("o_rest", G)
        proj_sum = count("proj_sum", TT)
        y_step = count("y_step", 2 * TT)
        base_ready = count("base_ready", TT)
        square_done = count("square_done", TT)
        ssq_ready = count("ssq_ready", 1)
        rms2_ready = count("rms2_ready", 1)
        y_ready = count("y_ready", TT)
        logit_sum = count("logit_sum", 1)
        logit_copied = count("logit_copied", 1)
        logit_turned = count("logit_turned", 1)
        logit_read = count("logit_read", TT, TT)
        base_stored = count("base_stored", 16, 16)
        xt_stored = count("xt_stored", 16, 16)
        comb_stored = count("comb_stored", 16, 16)
        pick_step = count("pick_step", 8)
        diff_ready = count("diff_ready", 1)
        diff_exp = count("diff_exp", 1)
        comb_ready = count("comb_ready", 1)

        x_src = x1_dram.rearrange("b (t p) c -> b p t c", p=P)
        next_x = x_src[1:B]
        base_dst = base_dram.rearrange("b (t p) c -> b p t c", p=P)
        wq_src = w_q.rearrange("(k p) n -> p k n", p=P)
        wq_raw = [x_tok[:].rearrange("p (k x) c -> p k (x c)", k=2),
                  prob[:, 0].rearrange("p (k x) c -> p k (x c)", k=2)]
        wo_src = w_o.rearrange("(g h c) n -> g h c n", h=HG, c=D)
        kva_raw = prob[:, 1, 0, 0:KC * (R + HD)].rearrange("p (k n) -> p k n", k=KC)
        kvb_raw = prob[0:R, 1, 1, :]
        mask_raw = prob[:, 1, 2, 0:2 * P].rearrange("p (m c) -> p m c", m=2)

        def by_channel(w):
            return w.rearrange("p (g d h) -> p g h d", h=HG, d=HD)

        def by_head(w):
            return w.rearrange("p (g h d) -> p g h d", h=HG, d=HD)

        splits = [(0, wq_raw[0], wq[:, 0, 0:2], wq[:, 1, 0:2]),
                  (1, wq_raw[1], wq[:, 0, 2:4], wq[:, 1, 2:4]),
                  (2, v[:], wo[:, 0], wo[:, 1])]
        splits += [(3, kva_raw[:, :, a:b], wkva[:, 0, :, c:c + b - a], wkva[:, 1, :, c:c + b - a])
                   for a, b, c in ((0, R, 0), (R, R + J, R), (R + J, R + HD, 96))]
        splits += [(3, by_head(kvb_raw), by_channel(wkvb_k[:, 0]), by_channel(wkvb_k[:, 1])),
                   (3, kvb_raw, wkvb_v[:, 0], wkvb_v[:, 1]),
                   (3, gate_raw[:], wgate[:, 0], wgate[:, 1])]

        def turns(eng, turn):
            with eng.Fori(0, B - 1) as i:
                turn(i, False)
            turn(B - 1, True)

        def in_stack(counts, i, g, pieces=PIECES):
            return counts[g % 2].sem, counts[g % 2].at(i, pieces * 16 * (g // 2 + 1))

        block = ctx.enter_context(nc.Block())

        @block.sync
        def _(sp):
            for n in range(2):
                sp.dma_start(wq_raw[n], wq_src[:, 2 * n:2 * n + 2, :]).then_inc(w_in[n], 16)
            for g in range(G):
                sp.dma_start(v[:, g, :], wo_src[g, :, 0:HD, :]).then_inc(w_in[2], 16)
            sp.dma_start(kva_raw, w_kva.rearrange("(k p) n -> p k n", p=P)).then_inc(w_in[3], 16)
            sp.dma_start(kvb_raw, w_kvb).then_inc(w_in[3], 16)
            sp.dma_start(gate_raw[:], w_gate.rearrange("(k p) n -> p k n", p=P)).then_inc(w_in[3], 16)
            sp.dma_start(cs[:], angles.rearrange("a p n -> p a n")).then_inc(angles_in, 16)
            sp.wait_ge(w_rest, len(splits))
            sp.dma_start(x_tok[:], x_src[0]).then_inc(x_in.sem, 16)

            def q_pieces(i, g):
                if g < 2:
                    sp.wait_ge(qk_rest.sem, qk_rest.at(i, 2 * g + 1))
                else:
                    sp.wait_ge(score_sum.sem, score_sum.at(i, (g - 1) * TT * HG))
                for piece, part in enumerate((0, 0, 1)):
                    sp.dma_start(q_stack[HD * piece:HD * (piece + 1), g % 2, :, :].bitcast(F32),
                                 qk[:, 0, part, :].bitcast(F32)).then_inc(q_in[g % 2].sem, 16)

            def k_pieces(i, g):
                sp.wait_ge(qk_rest.sem, qk_rest.at(i, 2 * g + 2))
                for piece, part in enumerate((0, 1, 0)):
                    sp.dma_start(k_stack[HD * piece:HD * (piece + 1), g % 2, :, :].bitcast(F32),
                                 qk[:, 1, part, :].bitcast(F32)).then_inc(k_in[g % 2].sem, 16)

            def rotated_pieces(i, g):
                s = g % 2
                sp.wait_ge(rope_rest.sem, rope_rest.at(i, 2 * (g // 2) + 2))
                for e in range(2):
                    for piece, part in enumerate((0, 0, 1)):
                        row0 = HD * piece + J * e
                        sp.dma_start(qr_stack[row0:row0 + J, s, :, :].bitcast(F32),
                                     rope[64 * s:64 * (s + 1), e, part, :].bitcast(F32)
                                     ).then_inc(rotated_in[s].sem, 16)

            def next_krope(i):
                sp.wait_ge(krope_rest.sem, krope_rest.at(i, 2))
                for e in range(2):
                    for piece, part in enumerate((0, 1, 0)):
                        row0 = HD * piece + J * e
                        sp.dma_start(kr_stack[row0:row0 + J, :].bitcast(F32),
                                     rope_k[e][part].bitcast(F32)).then_inc(krope_in.sem, 16)

            def next_groups(i):
                q_pieces(i, 0)
                k_pieces(i, 0)
                rotated_pieces(i, 0)
                next_krope(i)
                rotated_pieces(i, 1)
                q_pieces(i, 1)
                k_pieces(i, 1)

            def next_angles(i, passed=lambda: None):
                sp.wait_ge(h_ready.sem, h_ready.at(i, TT))
                for a in range(2):
                    sp.dma_start(csk[:, a], angles[a, 0:P // 2:HG, :]).then_inc(csk_in.sem, 16)
                    if a == 0:
                        passed()

            for stage in (next_angles, next_groups):
                stage(0)

            def turn(i, last):
                def row(g):
                    sp.wait_ge(row_ready.sem, row_ready.at(i, g + 1))
                    sp.dma_start(q_stack[96:97, g % 2, :, :].bitcast(F32),
                                 max_row[:, g % 2, :].bitcast(F32)).then_inc(row_in[g % 2].sem, 16)

                row(0)
                if not last:
                    sp.dma_start(x_tok[:], next_x[i]).then_inc(x_in.sem, 16)
                for g in range(2, G):
                    q_pieces(i, g)
                    rotated_pieces(i, g)
                    row(g - 1)
                    k_pieces(i, g)
                row(G - 1)
                def prob_read():
                    sp.wait_ge(pv_done.sem, pv_done.at(i, TT * G))

                if last:
                    prob_read()
                else:
                    next_angles(i + 1, prob_read)
                sp.dma_start(x_back, x_src[i]).then_inc(x_again.sem, 16)
                wait_apart(sp, base_ready.sem, base_ready.at(i, TT), w_rest)
                sp.dma_start(base_dst[i], x_back).then_inc(base_stored.sem, 16)
                if not last:
                    next_groups(i + 1)
                wait_apart(sp, y_rest.sem, y_rest.at(i, KC), w_rest)
                sp.dma_start(xt_dram[i], yT[:].bitcast(F32)).then_inc(xt_stored.sem, 16)
                wait_apart(sp, comb_ready.sem, comb_ready.at(i, 1), w_rest)
                sp.dma_start(comb_dram[i], comb[:]).then_inc(comb_stored.sem, 16)

            turns(sp, turn)
            sp.wait_ge(base_stored.sem, base_stored.at(B, 0))
            sp.wait_ge(xt_stored.sem, xt_stored.at(B, 0))
            sp.wait_ge(comb_stored.sem, comb_stored.at(B, 0))

        @block.gpsimd
        def _(pool):
            for dst, src in ((tg[:, 0:1], gate.partition_broadcast(P)), (ebias[:], e_bias.partition_broadcast(P)),
                             (w1[:], w_ln1),
                             (w2[:], w_ln2)):
                pool.dma_start(dst, src).then_inc(small_in, 16)
            nc.gpsimd.iota(expert[:], pattern=[[1, E]], base=0, channel_multiplier=0,
                           allow_small_or_imprecise_dtypes=True).then_inc(mask_step, 1)
            pool.wait_ge(mask_step, 1)
            nc.gpsimd.memset(ident[:], 0.0).then_inc(mask_step, 1)
            pool.wait_ge(mask_step, 2)
            nc.gpsimd.memset(mask_raw, 0.0).then_inc(mask_step, 1)
            pool.wait_ge(mask_step, 3)
            nc.gpsimd.affine_select(out=ident[:], in_=ident[:], compare_op=ALU.not_equal, fill=1.0, base=0,
                                    pattern=[[-1, P]], channel_multiplier=1).then_inc(mask_step, 1)
            pool.wait_ge(mask_step, 4)
            nc.gpsimd.affine_select(out=mask_raw[:, 0], in_=mask_raw[:, 0], compare_op=ALU.is_ge, fill=BIG, base=0,
                                    pattern=[[-1, P]], channel_multiplier=1).then_inc(mask_step, 1)
            pool.wait_ge(mask_step, 5)
            nc.gpsimd.affine_select(out=mask_raw[:, 1], in_=mask_raw[:, 1], compare_op=ALU.is_ge, fill=BIG, base=0,
                                    pattern=[[1, P]], channel_multiplier=-1).then_inc(const_ready, 1)
            pool.wait_ge(fill_ready, 1)
            pool.sem_inc(base_stored.sem, 16)
            pool.sem_inc(xt_stored.sem, 16)
            pool.sem_inc(comb_stored.sem, 16)

            def next_powers(i):
                pool.wait_ge(var_ready.sem, var_ready.at(i, 1))
                nc.gpsimd.tensor_tensor(stat[:, 1], stat[:, 0], mhalf[:], ALU.pow).then_inc(rstd_ready.sem, 1)
                pool.wait_ge(ms_ready.sem, ms_ready.at(i, 1))
                nc.gpsimd.tensor_tensor(stat[:, 4], stat[:, 3], mhalf[:], ALU.pow).then_inc(rms_ready.sem, 1)

            def next_krope(i):
                even, odd, res, aux = krope[:, 0, :], krope[:, 1, :], krope_work[:, 0, :], krope_work[:, 1, :]
                cos, sin = csk[:, 0], csk[:, 1]
                pool.wait_ge(lat_main.sem, lat_main.at(i, 3))
                pool.wait_ge(csk_in.sem, csk_in.at(i, 2 * 16))
                nc.gpsimd.tensor_tensor(res, even, cos, ALU.mult).then_inc(krope_step.sem, 1)
                pool.wait_ge(krope_step.sem, krope_step.at(i, 1))
                nc.gpsimd.tensor_tensor(aux, odd, sin, ALU.mult).then_inc(krope_step.sem, 1)
                pool.wait_ge(krope_step.sem, krope_step.at(i, 2))
                nc.gpsimd.tensor_tensor(res, res, aux, ALU.subtract).then_inc(krope_step.sem, 1)
                pool.wait_ge(krope_step.sem, krope_step.at(i, 3))
                nc.gpsimd.tensor_tensor(aux, even, sin, ALU.mult).then_inc(krope_step.sem, 1)
                pool.wait_ge(krope_step.sem, krope_step.at(i, 4))
                pool.wait_ge(krope_main.sem, krope_main.at(i, 1))
                nc.gpsimd.tensor_tensor(rope_k[0][1], res, rope_k[0][0].bitcast(F32),
                                        ALU.subtract).then_inc(krope_rest.sem, 1)
                pool.wait_ge(krope_rest.sem, krope_rest.at(i, 1))
                nc.gpsimd.tensor_tensor(res, odd, cos, ALU.mult).then_inc(krope_step.sem, 1)
                pool.wait_ge(krope_step.sem, krope_step.at(i, 5))
                nc.gpsimd.tensor_tensor(res, res, aux, ALU.add).then_inc(krope_step.sem, 1)
                pool.wait_ge(krope_main.sem, krope_main.at(i, 2))
                nc.gpsimd.tensor_tensor(rope_k[1][1], res, rope_k[1][0].bitcast(F32),
                                        ALU.subtract).then_inc(krope_rest.sem, 1)
                pool.wait_ge(krope_rest.sem, krope_rest.at(i, 2))

            next_powers(0)
            pool.wait_ge(rms_ready.sem, rms_ready.at(0, 1))
            next_krope(0)

            def turn(i, last):
                for g in range(G):
                    if g == G - 1 and not last:
                        next_powers(i + 1)
                    pool.wait_ge(o_main.sem, o_main.at(i, g + 1))
                    nc.gpsimd.tensor_tensor(oT[:, 1, g, :], o_norm[:], oT[:, 0, g, :].bitcast(F32),
                                            ALU.subtract).then_inc(o_rest.sem, 1)
                pool.wait_ge(ssq_ready.sem, ssq_ready.at(i, 1))
                nc.gpsimd.tensor_tensor(ssq[:, 2], ssq[:, 1], mhalf[:], ALU.pow).then_inc(rms2_ready.sem, 1)
                if not last:
                    pool.wait_ge(rms2_ready.sem, rms2_ready.at(i, 1))
                    next_krope(i + 1)

            turns(pool, turn)

        @block.scalar
        def _(act):
            act.wait_ge(small_in, 4 * 16)
            nc.scalar.activation(tg[:, 1:2], tg[:, 0:1], ACT.Tanh).then_inc(tg_ready, 1)
            act.wait_ge(kva_zero, 1)
            for n, raw, main, _ in splits:
                act.wait_ge(w_in[n], (16, 16, 64, 48)[n])
                nc.scalar.activation(main, raw, ACT.Copy).then_inc(w_main, 1)

            def turn_mains(i, dst, banks, w, done, main):
                for k in range(KC):
                    act.wait_ge(done.sem, done.at(i, k + 1))
                    nc.scalar.activation(dst[:, 0, k, :], bank[banks[k]], ACT.Copy,
                                         scale=w[:, k:k + 1]).then_inc(main.sem, 1)

            def qk_main_of(i, g, w):
                act.wait_ge(qk_sum.sem, qk_sum.at(i, 2 * g + w + 1))
                if g:
                    act.wait_ge(*in_stack((q_in, k_in)[w], i, g - 1))
                nc.scalar.activation(qk[:, w, 0, :], bank[QK_BANK[g][w]], ACT.Copy).then_inc(qk_main.sem, 1)

            def rope_main_of(i, n, e):
                if n and not e:
                    for g in range(2):
                        act.wait_ge(*in_stack(rotated_in, i, g, 2 * PIECES))
                act.wait_ge(rope_step.sem, rope_step.at(i, 6 * n + (3, 6)[e]))
                nc.scalar.activation(rope[:, e, 0, :], tmp[:], ACT.Copy).then_inc(rope_main.sem, 1)

            def next_input(i):
                turn_mains(i, hT, TURN_BANK, w1, turned, turned_main)

            def next_latent(i):
                act.wait_ge(lat_sum.sem, lat_sum.at(i, 1))
                nc.scalar.activation(lat[:, 0, :], bank[4][0:R], ACT.Copy).then_inc(lat_main.sem, 1)
                for e in range(2):
                    row0 = (R, 96)[e]
                    nc.scalar.activation(krope[:, e, :], bank[4][row0:row0 + J], ACT.Copy).then_inc(lat_main.sem, 1)

            def krope_main_of(i, e):
                act.wait_ge(krope_step.sem, krope_step.at(i, (3, 6)[e]))
                nc.scalar.activation(rope_k[e][0], krope_work[:, 0, :], ACT.Copy).then_inc(krope_main.sem, 1)

            def next_group0(i):
                qk_main_of(i, 0, 0)
                qk_main_of(i, 0, 1)

            def next_groups(i):
                krope_main_of(i, 0)
                rope_main_of(i, 0, 0)
                for t in range(TT):
                    act.wait_ge(v_sum.sem, v_sum.at(i, t + 1))
                    nc.scalar.activation(v[:, t, :], bank[2 + t % 2], ACT.Copy).then_inc(v_ready.sem, 1)
                rope_main_of(i, 0, 1)
                krope_main_of(i, 1)
                qk_main_of(i, 1, 0)
                qk_main_of(i, 1, 1)

            for stage in (next_input, next_latent, next_group0, next_groups):
                stage(0)

            def turn(i, last):
                def output_main(g):
                    act.wait_ge(o_ready.sem, o_ready.at(i, g + 1))
                    if g == 0:
                        act.wait_ge(xt_stored.sem, xt_stored.at(i, 0))
                    nc.scalar.activation(oT[:, 0, g, :], o_norm[:], ACT.Copy).then_inc(o_main.sem, 1)

                rope_main_of(i, 1, 0)
                rope_main_of(i, 1, 1)
                qk_main_of(i, 2, 0)
                for g in range(G):
                    for k in range(TT):
                        for h in range(HG):
                            n = (g * TT + k) * HG + h
                            act.wait_ge(score_sum.sem, score_sum.at(i, n + 1))
                            if n == HG:
                                act.wait_ge(base_stored.sem, base_stored.at(i, 0))
                            if n >= 2 * HG:
                                act.wait_ge(pv_done.sem, pv_done.at(i, n // HG - 1))
                            nc.scalar.activation(prob[:, k % 2, h, k * P:], bank[h][:, 0:T - k * P], ACT.Exp,
                                                 scale=SCALE).then_inc(exp_done.sem, 1)
                        if k == 0 and g:
                            output_main(g - 1)
                        if k == 0 and g == 1:
                            qk_main_of(i, 3, 0)
                    if g + 2 < G:
                        qk_main_of(i, g + 2, 1)
                if not last:
                    next_input(i + 1)
                output_main(G - 1)
                if not last:
                    next_latent(i + 1)
                for t in range(TT):
                    act.wait_ge(y_step.sem, y_step.at(i, TT + t + 1))
                    nc.scalar.activation(bank[t], y2[:, t], ACT.Square,
                                         accum_out=ssq[:, 0, t:t + 1]).then_inc(square_done.sem, 1)
                if not last:
                    next_group0(i + 1)
                turn_mains(i, yT, range(KC), w2, y_turned, y_main)
                act.wait_ge(logit_sum.sem, logit_sum.at(i, 1))
                nc.scalar.activation(logit_row, bank[0][0:E, :], ACT.Copy).then_inc(logit_copied.sem, 1)
                if not last:
                    next_groups(i + 1)
                act.wait_ge(diff_ready.sem, diff_ready.at(i, 1))
                nc.scalar.activation(pick[:, 1], pick[:, 0], ACT.Exp).then_inc(diff_exp.sem, 1)

            turns(act, turn)

        @block.vector
        def _(dve):
            nc.vector.memset(mhalf[:], -0.5).then_inc(fill_ready, 1)
            nc.vector.memset(ones[:], 1.0).then_inc(fill_ready, 1)
            nc.vector.memset(wkva[:].bitcast(F32), 0.0).then_inc(kva_zero, 1)
            nc.vector.memset(k_stack[96:97, :, :, :].bitcast(F32), 1.0).then_inc(fill_ready, 1)
            dve.wait_ge(kva_zero, 1)
            for n, (_, raw, main, rest) in enumerate(splits):
                dve.wait_ge(w_main, n + 1)
                nc.vector.tensor_tensor(rest, raw, main.bitcast(F32), ALU.subtract).then_inc(w_rest, 1)
            dve.wait_ge(const_ready, 1)
            dve.wait_ge(tg_ready, 1)
            dve.wait_ge(angles_in, 16)
            nc.vector.tensor_copy(ident_r[:], ident[:])
            nc.vector.tensor_copy(mask_q[:], mask_raw[:, 0])
            nc.vector.tensor_copy(mask_k[:], mask_raw[:, 1]).then_inc(fill_ready, 1)
            dve.sem_inc(logit_read.sem, TT)

            def next_norms(i):
                steps = [0]

                def stat_of(ins):
                    steps[0] += 1
                    ins.then_inc(stat_step.sem, 1)
                    dve.wait_ge(stat_step.sem, stat_step.at(i, steps[0]))

                dve.wait_ge(x_in.sem, x_in.at(i, 16))
                for t in range(TT):
                    nc.vector.bn_stats(st6[:, t], x_tok[:, t]).then_inc(stat_step.sem, 1)
                steps[0] = TT
                wait_by_memset(nc, stat_step.sem, stat_step.at(i, TT), waited[:])
                for t in range(TT - 1):
                    nc.vector.bn_aggr(mv[:, t], st6[:, t])
                stat_of(nc.vector.bn_aggr(mv[:, TT - 1], st6[:, TT - 1]))
                nc.vector.tensor_scalar(stat[:, 0], mv[:, :, 1], EPS, None, ALU.add).then_inc(var_ready.sem, 1)
                dve.wait_ge(rstd_ready.sem, rstd_ready.at(i, 1))
                stat_of(nc.vector.tensor_tensor(stat[:, 2], stat[:, 1], stat[:, 1], ALU.mult))
                stat_of(nc.vector.tensor_tensor(stat[:, 3], stat[:, 2], mv[:, :, 1], ALU.mult))
                nc.vector.tensor_scalar(stat[:, 3], stat[:, 3], EPS, None, ALU.add).then_inc(ms_ready.sem, 1)
                dve.wait_ge(rms_ready.sem, rms_ready.at(i, 1))
                stat_of(nc.vector.tensor_tensor(stat[:, 5], stat[:, 1], stat[:, 4], ALU.mult))

            def next_normalise(i):
                for t in range(TT):
                    nc.vector.tensor_scalar(xn[:, t], x_tok[:, t], mv[:, t, 0:1], stat[:, 5, t:t + 1],
                                            ALU.subtract, ALU.mult).then_inc(h_ready.sem, 1)

            def turn_rests(i, dst, banks, w, main, rest):
                for k in range(KC):
                    dve.wait_ge(main.sem, main.at(i, k + 1))
                    nc.vector.scalar_tensor_tensor(out=dst[:, 1, k, :], in0=bank[banks[k]], scalar=w[:, k:k + 1],
                                                   in1=dst[:, 0, k, :].bitcast(F32), op0=ALU.mult,
                                                   op1=ALU.subtract).then_inc(rest.sem, 1)

            def rotate(i, even, odd, cos, sin, res, aux, step, at, main_ready, dst, rest_done):
                nc.vector.tensor_tensor(res, even, cos, ALU.mult).then_inc(step.sem, 1)
                nc.vector.tensor_tensor(aux, odd, sin, ALU.mult).then_inc(step.sem, 1)
                dve.wait_ge(step.sem, step.at(i, at + 2))
                nc.vector.tensor_tensor(res, res, aux, ALU.subtract).then_inc(step.sem, 1)
                dve.wait_ge(step.sem, step.at(i, at + 3))
                nc.vector.tensor_tensor(aux, even, sin, ALU.mult).then_inc(step.sem, 1)
                main_ready(0)
                nc.vector.tensor_tensor(dst(0, 1), res, dst(0, 0).bitcast(F32),
                                        ALU.subtract).then_inc(rest_done.sem, 1)
                dve.wait_ge(rest_done.sem, rest_done.at(i, 2 * (at // 6) + 1))
                nc.vector.tensor_tensor(res, odd, cos, ALU.mult).then_inc(step.sem, 1)
                dve.wait_ge(step.sem, step.at(i, at + 5))
                nc.vector.tensor_tensor(res, res, aux, ALU.add).then_inc(step.sem, 1)
                dve.wait_ge(step.sem, step.at(i, at + 6))
                main_ready(1)
                nc.vector.tensor_tensor(dst(1, 1), res, dst(1, 0).bitcast(F32),
                                        ALU.subtract).then_inc(rest_done.sem, 1)
                dve.wait_ge(rest_done.sem, rest_done.at(i, 2 * (at // 6) + 2))

            def rope_of(i, n):
                dve.wait_ge(rope_sum.sem, rope_sum.at(i, 2 * n + 2))
                rotate(i, bank[ROPE_BANKS[n][0]], bank[ROPE_BANKS[n][1]], cs[:, 0], cs[:, 1], tmp[:], o_norm[:],
                       rope_step, 6 * n,
                       lambda e: dve.wait_ge(rope_main.sem, rope_main.at(i, 2 * n + e + 1)),
                       lambda e, part: rope[:, e, part, :], rope_rest)

            def qk_rest_of(i, g, w):
                dve.wait_ge(qk_main.sem, qk_main.at(i, 2 * g + w + 1))
                nc.vector.tensor_tensor(qk[:, w, 1, :], bank[QK_BANK[g][w]], qk[:, w, 0, :].bitcast(F32),
                                        ALU.subtract).then_inc(qk_rest.sem, 1)

            def next_input(i):
                turn_rests(i, hT, TURN_BANK, w1, turned_main, turned_rest)

            def next_latent(i):
                dve.wait_ge(lat_main.sem, lat_main.at(i, 1))
                nc.vector.tensor_tensor(lat[:, 1, :], bank[4][0:R], lat[:, 0, :].bitcast(F32),
                                        ALU.subtract).then_inc(lat_rest.sem, 1)

            def next_group0(i):
                qk_rest_of(i, 0, 0)
                qk_rest_of(i, 0, 1)

            def next_groups(i):
                rope_of(i, 0)
                qk_rest_of(i, 1, 0)
                qk_rest_of(i, 1, 1)

            for stage in (next_norms, next_normalise, next_input, next_latent, next_group0, next_groups):
                stage(0)

            def turn(i, last):
                def maxima(g, t):
                    for h in range(HG):
                        n = (g * TT + t) * HG + h
                        dve.wait_ge(max_sum.sem, max_sum.at(i, n + 1))
                        nc.vector.tensor_reduce(neg_max[:, g % 2, h * TT + t:h * TT + t + 1],
                                                bank[4 + n % 2][:, 0:(t + 1) * P], AX_X, ALU.max,
                                                negate=True).then_inc(max_done.sem, 1)

                def rows(g):
                    dve.wait_ge(max_turned.sem, max_turned.at(i, g + 1))
                    nc.vector.tensor_copy(max_row[:, g % 2, :], bank[0][0:HG * TT, 0:P]).then_inc(row_ready.sem, 1)

                maxima(0, 0)
                maxima(0, 1)
                rope_of(i, 1)
                maxima(0, 2)
                maxima(0, 3)
                rows(0)
                qk_rest_of(i, 2, 0)
                for g in range(G):
                    if g == 1:
                        qk_rest_of(i, 3, 0)
                    if g + 1 < G:
                        for t in range(TT):
                            maxima(g + 1, t)
                        rows(g + 1)
                    else:
                        nc.vector.tensor_copy(kept[:, 0], mv[:, :, 0])
                        nc.vector.tensor_copy(kept[:, 1], stat[:, 1]).then_inc(kept_ready.sem, 1)
                        dve.wait_ge(kept_ready.sem, kept_ready.at(i, 1))
                        if not last:
                            next_norms(i + 1)
                            dve.wait_ge(pv_done.sem, pv_done.at(i, TT * G - 1))
                            next_normalise(i + 1)
                    dve.wait_ge(pv_done.sem, pv_done.at(i, TT * (g + 1)))
                    if g:
                        dve.wait_ge(o_rest.sem, o_rest.at(i, g))
                    nc.vector.reciprocal(o_norm[:], bank[7]).then_inc(recip_done.sem, 1)
                    if g + 2 < G:
                        qk_rest_of(i, g + 2, 1)
                    dve.wait_ge(recip_done.sem, recip_done.at(i, g + 1))
                    nc.vector.tensor_tensor(o_norm[:], bank[6], o_norm[:], ALU.mult).then_inc(o_ready.sem, 1)
                if not last:
                    next_input(i + 1)
                dve.wait_ge(x_again.sem, x_again.at(i, 16))
                for t in range(TT):
                    nc.vector.tensor_scalar(y2[:, t], x_back[:, t], kept[:, 0, t:t + 1], kept[:, 1, t:t + 1],
                                            ALU.subtract, ALU.mult).then_inc(y_step.sem, 1)
                for t in range(TT):
                    dve.wait_ge(proj_sum.sem, proj_sum.at(i, t + 1))
                    if t == 0:
                        dve.wait_ge(y_step.sem, y_step.at(i, TT))
                    nc.vector.tensor_tensor(y2[:, t], bank[t], y2[:, t], ALU.add).then_inc(y_step.sem, 1)
                if not last:
                    next_latent(i + 1)
                for t in range(TT):
                    dve.wait_ge(y_step.sem, y_step.at(i, TT + t + 1))
                    nc.vector.scalar_tensor_tensor(out=x_back[:, t], in0=y2[:, t], scalar=tg[:, 1:2],
                                                   in1=x_back[:, t], op0=ALU.mult,
                                                   op1=ALU.add).then_inc(base_ready.sem, 1)
                dve.wait_ge(square_done.sem, square_done.at(i, TT))
                nc.vector.tensor_scalar(ssq[:, 1], ssq[:, 0], 1.0 / C, EPS, ALU.mult,
                                        ALU.add).then_inc(ssq_ready.sem, 1)
                dve.wait_ge(rms2_ready.sem, rms2_ready.at(i, 1))
                dve.wait_ge(base_ready.sem, base_ready.at(i, TT))
                for t in range(TT):
                    nc.vector.tensor_scalar(y2[:, t], y2[:, t], ssq[:, 2, t:t + 1], None,
                                            ALU.mult).then_inc(y_ready.sem, 1)
                if not last:
                    next_group0(i + 1)
                turn_rests(i, yT, range(KC), w2, y_main, y_rest)
                if not last:
                    next_groups(i + 1)

                picks = [0]

                def pick_of(ins):
                    picks[0] += 1
                    ins.then_inc(pick_step.sem, 1)
                    wait_by_memset(nc, pick_step.sem, pick_step.at(i, picks[0]), waited[:])

                dve.wait_ge(logit_turned.sem, logit_turned.at(i, 1))
                for t in range(TT):
                    nc.vector.tensor_tensor(logit[:, t], bank[0][:, t * E:(t + 1) * E], ebias[:],
                                            ALU.add).then_inc(logit_read.sem, 1)
                wait_by_memset(nc, logit_read.sem, logit_read.at(i, TT), waited[:])
                for t in range(TT):
                    last = nc.vector.max(top[:, t], logit[:, t])
                pick_of(last)
                for t in range(TT):
                    last = nc.vector.max_index(index[:, t], top[:, t], logit[:, t])
                pick_of(last)
                pick_of(nc.vector.tensor_copy(index_f[:], index[:]))
                nc.vector.tensor_tensor(pick[:, 0], top[:, :, 1], top[:, :, 0], ALU.subtract
                                        ).then_inc(diff_ready.sem, 1)
                dve.wait_ge(diff_exp.sem, diff_exp.at(i, 1))
                pick_of(nc.vector.tensor_scalar(pick[:, 2], pick[:, 1], 1.0, None, ALU.add))
                pick_of(nc.vector.reciprocal(pick[:, 2], pick[:, 2]))
                pick_of(nc.vector.tensor_scalar(pick[:, 3], pick[:, 2], tg[:, 1:2], None, ALU.mult))
                pick_of(nc.vector.tensor_tensor(pick[:, 4], pick[:, 3], pick[:, 1], ALU.mult))
                for t in range(TT):
                    for r in range(2):
                        last = nc.vector.tensor_scalar(one_hot[:, r, t], expert[:], index_f[:, t, r:r + 1],
                                                       pick[:, 3 + r, t:t + 1], ALU.is_equal, ALU.mult)
                pick_of(last)
                dve.wait_ge(comb_stored.sem, comb_stored.at(i, 0))
                nc.vector.tensor_tensor(comb[:], one_hot[:, 0], one_hot[:, 1], ALU.add).then_inc(comb_ready.sem, 1)

            turns(dve, turn)

        @block.tensor
        def _(pe):
            pe.wait_ge(const_ready, 1)
            pe.wait_ge(fill_ready, 4)
            pe.wait_ge(w_rest, len(splits))

            def transposes(i, src, ready, banks, done):
                for k in range(KC):
                    for t in range(TT):
                        pe.wait_ge(ready.sem, ready.at(i, t + 1))
                        last = pe.transpose(bank[banks[k]][:, t * P:(t + 1) * P], src[:, t, k * P:(k + 1) * P],
                                            ident[:])
                    last.then_inc(done.sem, 1)

            def project(b, columns, done):
                split_sum(pe, bank[b], lambda a, k: wq[:, a, k, columns:columns + P],
                          lambda a, k: hT[:, a, k, :], range(KC)).then_inc(done.sem, 1)

            def project_q(g):
                project(QK_BANK[g][0], g * P, qk_sum)

            def project_k(g):
                split_sum(pe, bank[QK_BANK[g][1]], lambda a, k: wkvb_k[:, a, g * P:(g + 1) * P],
                          lambda a, k: lat[:, a, :], range(1)).then_inc(qk_sum.sem, 1)

            def project_rope(n, e):
                project(ROPE_BANKS[n][e], C + (2 * n + e) * P, rope_sum)

            def next_input(i):
                transposes(i, xn, h_ready, TURN_BANK, turned)

            def next_latent(i):
                pe.wait_ge(turned_rest.sem, turned_rest.at(i, KC))
                split_sum(pe, bank[4], lambda a, k: wkva[:, a, k, :], lambda a, k: hT[:, a, k, :],
                          range(KC)).then_inc(lat_sum.sem, 1)
                project_q(0)
                pe.wait_ge(lat_rest.sem, lat_rest.at(i, 1))
                project_k(0)
                project_rope(0, 0)

            def next_odd(i):
                pe.wait_ge(lat_main.sem, lat_main.at(i, 3))
                project_rope(0, 1)

            def next_values(i, tiles):
                for t in tiles:
                    if t >= 2:
                        pe.wait_ge(v_ready.sem, v_ready.at(i, t - 1))
                    split_sum(pe, bank[2 + t % 2], lambda a, k: lat[:, a, t * P:(t + 1) * P],
                              lambda a, k: wkvb_v[:, a, :], range(1)).then_inc(v_sum.sem, 1)

            def next_group1(i):
                pe.wait_ge(qk_rest.sem, qk_rest.at(i, 1))
                project_q(1)
                pe.wait_ge(qk_rest.sem, qk_rest.at(i, 2))
                project_k(1)

            for stage in (next_input, next_latent, next_odd):
                stage(0)
            next_values(0, range(TT))
            next_group1(0)

            def turn(i, last):
                def max_score(g, n):
                    t, h = n // HG, n % HG
                    n += g * TT * HG
                    out = bank[4 + n % 2]
                    if n >= 2:
                        pe.wait_ge(max_done.sem, max_done.at(i, n - 1))
                    s, w = g % 2, (t + 1) * P
                    pe.matmul(out[:, 0:w], q_stack[0:96, s, h, t * P:w], k_stack[0:96, s, h, 0:w],
                              start=True, stop=False)
                    pe.matmul(out[:, t * P:w], ident_r[:], mask_q[:], start=False, stop=False)
                    pe.matmul(out[:, 0:w], qr_stack[:, s, h, t * P:w], kr_stack[:, 0:w],
                              start=False, stop=True).then_inc(max_sum.sem, 1)

                def turn_max(g):
                    pe.wait_ge(max_done.sem, max_done.at(i, (g + 1) * TT * HG))
                    if g:
                        pe.wait_ge(exp_done.sem, exp_done.at(i, g * TT * HG))
                    pe.transpose(bank[0][0:HG * TT, 0:P], neg_max[:, g % 2, :], ident[:]).then_inc(max_turned.sem, 1)

                def scores(g, k, h):
                    n = (g * TT + k) * HG + h
                    if n >= HG:
                        pe.wait_ge(exp_done.sem, exp_done.at(i, n + 1 - HG))
                    s, w = g % 2, T - k * P
                    pe.matmul(bank[h][:, 0:w], k_stack[:, s, h, k * P:(k + 1) * P], q_stack[:, s, h, k * P:],
                              start=True, stop=False)
                    pe.matmul(bank[h][:, 0:P], ident_r[:], mask_k[:], start=False, stop=False)
                    pe.matmul(bank[h][:, 0:w], kr_stack[:, k * P:(k + 1) * P], qr_stack[:, s, h, k * P:],
                              start=False, stop=True).then_inc(score_sum.sem, 1)

                def weigh(g, k, sums):
                    if not sums:
                        pe.wait_ge(exp_done.sem, exp_done.at(i, (g * TT + k + 1) * HG))
                        if k == 0 and g:
                            pe.wait_ge(o_ready.sem, o_ready.at(i, g))
                    for h in range(HG):
                        out = bank[7 if sums else 6][HD * h:HD * (h + 1), k * P:]
                        c = g * P + h * HD
                        last = pe.matmul(out, ones[:] if sums else v[:, k, c:c + HD], prob[:, k % 2, h, k * P:],
                                         start=(k == 0), stop=(k == TT - 1))
                    if sums:
                        last.then_inc(pv_done.sem, 1)

                pe.wait_ge(v_ready.sem, v_ready.at(i, TT))
                project_rope(1, 0)
                project_rope(1, 1)
                pe.wait_ge(krope_in.sem, krope_in.at(i, 2 * PIECES * 16))
                pe.wait_ge(*in_stack(q_in, i, 0))
                pe.wait_ge(*in_stack(k_in, i, 0))
                pe.wait_ge(*in_stack(rotated_in, i, 0, 2 * PIECES))
                pe.wait_ge(rope_rest.sem, rope_rest.at(i, 2))
                pe.wait_ge(qk_rest.sem, qk_rest.at(i, 3))
                for n in range(TT * HG):
                    max_score(0, n)
                pe.wait_ge(logit_read.sem, logit_read.at(i, 0))
                turn_max(0)
                project_q(2)
                pe.wait_ge(rope_rest.sem, rope_rest.at(i, 4))
                pe.wait_ge(qk_rest.sem, qk_rest.at(i, 5))
                for g in range(G):
                    pe.wait_ge(row_in[g % 2].sem, row_in[g % 2].at(i, (g // 2 + 1) * 16))
                    n = 0
                    for step, maxima in enumerate(MAXIMA_STEPS[min(g, 1)]):
                        k, half = step // 2, step % 2
                        if n == 0 and maxima and g + 1 < G:
                            pe.wait_ge(*in_stack(q_in, i, g + 1))
                            pe.wait_ge(*in_stack(k_in, i, g + 1))
                            pe.wait_ge(*in_stack(rotated_in, i, g + 1, 2 * PIECES))
                            if g == 1:
                                pe.wait_ge(qk_rest.sem, qk_rest.at(i, 7))
                        for j in range(max(2, maxima)):
                            if k < TT and j < 2:
                                scores(g, k, 2 * half + j)
                            if j < maxima and g + 1 < G:
                                max_score(g + 1, n)
                                n += 1
                        if k:
                            weigh(g, k - 1, half == 1)
                    if g + 1 < G:
                        turn_max(g + 1)
                    if g + 2 < G:
                        project_k(g + 2)
                    if g == 0:
                        project_q(3)
                if not last:
                    next_input(i + 1)
                pe.wait_ge(o_rest.sem, o_rest.at(i, G))
                for t in range(TT):
                    if t >= 2 and not last:
                        pe.wait_ge(turned_rest.sem, turned_rest.at(i + 1, t + 1))
                    split_sum(pe, bank[t], lambda a, k: oT[:, a, k, t * P:(t + 1) * P],
                              lambda a, k: wo[:, a, k, :], range(G)).then_inc(proj_sum.sem, 1)
                if not last:
                    next_latent(i + 1)
                transposes(i, y2, y_ready, range(KC), y_turned)
                if not last:
                    next_odd(i + 1)
                pe.wait_ge(y_rest.sem, y_rest.at(i, KC))
                split_sum(pe, bank[0][0:E, :], lambda a, k: wgate[:, a, k, :], lambda a, k: yT[:, a, k, :],
                          range(KC)).then_inc(logit_sum.sem, 1)
                pe.wait_ge(logit_copied.sem, logit_copied.at(i, 1))
                if not last:
                    next_values(i + 1, (0,))
                for t in range(TT):
                    last_tile = pe.transpose(bank[0][:, t * E:(t + 1) * E], logit_row[:, t * P:(t + 1) * P],
                                             ident[0:E, 0:E])
                last_tile.then_inc(logit_turned.sem, 1)
                if not last:
                    next_values(i + 1, range(1, TT))
                    next_group1(i + 1)

            turns(pe, turn)


def experts(nc, banks, base_dram, xt_dram, comb_dram, w_gate, w_up, w_down, s_gate, s_up, s_down, gate, out):
    E, _, I = w_gate.shape
    S = s_gate.shape[0]
    IC = I // P
    HALVES = 2
    NB = B // HALVES
    STEPS = HALVES * (E + S)
    W = 2 * KC * I + IC * C
    assert S == 1 and E % 2 == 0
    with ExitStack() as ctx:
        def sb(name, shape, dt=F32):
            return ctx.enter_context(nc.sbuf_tensor("c_" + name, shape, dt))

        def count(name, per_step, credit=0):
            return Count(ctx, nc, "c_" + name, per_step, credit)

        xT = sb("xT", [P, NB, 2, KC, T], F32R)
        acc = sb("acc", [P, NB, TT, C])
        raw = sb("raw", [P, W])
        weights = sb("weights", [P, 2, 2, W], F32R)
        silu = sb("silu", [P, IC, T])
        hidden = sb("hidden", [P, IC, T])
        hT = sb("hT", [P, 2, 2, IC, T], F32R)
        comb = sb("comb", [P, B, TT, E])
        unit = sb("unit", [P, NB, TT])
        scale = sb("scale", [P, 2, NB, TT])
        tg = sb("tg", [P, 2])

        comb_in = ctx.enter_context(nc.semaphore("c_comb_in"))
        gate_in = ctx.enter_context(nc.semaphore("c_gate_in"))
        const_ready = ctx.enter_context(nc.semaphore("c_const_ready"))
        x_in = [ctx.enter_context(nc.semaphore(f"c_x_in{b}")) for b in range(NB)]
        acc_in = [ctx.enter_context(nc.semaphore(f"c_acc_in{b}")) for b in range(NB)]
        stored = [ctx.enter_context(nc.semaphore(f"c_stored{b}")) for b in range(NB)]
        raw_in = count("raw_in", 3 * 16)
        w_main = count("w_main", 1)
        w_rest = count("w_rest", 1, 1)
        scale_ready = count("scale_ready", 1)
        gate_sum = count("gate_sum", NB)
        up_sum = count("up_sum", NB)
        silu_done = count("silu_done", NB)
        hidden_done = count("hidden_done", NB)
        h_main = count("h_main", NB)
        h_rest = count("h_rest", NB)
        down_sum = count("down_sum", NB * TT)
        added = count("added", NB * TT)

        x_src = xt_dram
        acc_src = base_dram.rearrange("b (t p) c -> b p t c", p=P)
        out_dst = out.rearrange("b (t p) c -> b p t c", p=P)
        G0, U0, D0 = 0, KC * I, 2 * KC * I

        def gate_up(s, part, up, k, j):
            return weights[:, s, part, (U0 if up else G0) + k * I + j * P:(U0 if up else G0) + k * I + (j + 1) * P]

        def down(s, part, j):
            return weights[:, s, part, D0 + j * C:D0 + (j + 1) * C]

        block = ctx.enter_context(nc.Block())

        @block.sync
        def _(sp):
            def load_weights(step, g, u, d):
                wait_apart(sp, w_rest.sem, w_rest.at(step, 0), w_rest.sem)
                for w, at, n in ((g, G0, KC), (u, U0, KC), (d, D0, IC)):
                    size = n * (I if n == KC else C)
                    sp.dma_start(raw[:, at:at + size].rearrange("p (k n) -> p k n", k=n),
                                 w.rearrange("(k p) n -> p k n", p=P)).then_inc(raw_in.sem, 16)

            def load_batches(half):
                for b in range(NB):
                    if half:
                        sp.wait_ge(up_sum.sem, NB * E + b + 1)
                    sp.dma_start(xT[:, b].bitcast(F32), x_src[half * NB + b]).then_inc(x_in[b], 16)
                    if half:
                        sp.wait_ge(added.sem, TT * (NB * E + b + 1))
                        sp.dma_start(out_dst[b], acc[:, b]).then_inc(stored[b], 16)
                        sp.wait_ge(stored[b], 16)
                    sp.dma_start(acc[:, b], acc_src[half * NB + b]).then_inc(acc_in[b], 16)

            load_weights(0, s_gate[0], s_up[0], s_down[0])
            sp.dma_start(comb[:], comb_dram.rearrange("b p t e -> p b t e")).then_inc(comb_in, 16)
            load_batches(0)
            with sp.Fori(0, E) as e:
                load_weights(e + 1, w_gate[e], w_up[e], w_down[e])
            load_weights(E + 1, w_gate[0], w_up[0], w_down[0])
            load_batches(1)
            with sp.Fori(1, E) as e:
                load_weights(e + E + 1, w_gate[e], w_up[e], w_down[e])
            load_weights(STEPS - 1, s_gate[0], s_up[0], s_down[0])
            for b in range(NB):
                sp.wait_ge(added.sem, TT * (NB * (STEPS - 1) + b + 1))
                sp.dma_start(out_dst[NB + b], acc[:, b]).then_inc(stored[b], 16)
            for b in range(NB):
                sp.wait_ge(stored[b], 32)

        def order(eng, step):
            step(0, 0, 0, None)
            for half, first in ((0, 1), (1, E + 1)):
                with eng.Fori(0, E // 2) as e:
                    step(2 * e + first, 1, half, 2 * e)
                    step(2 * e + (first + 1), 0, half, 2 * e + 1)
            step(STEPS - 1, 1, 1, None)

        def is_first(half, e):
            return half == 0 and e is None

        def is_last(half, e):
            return half == 1 and e is None

        @block.gpsimd
        def _(pool):
            pool.dma_start(tg[:, 0:1], gate.partition_broadcast(P)).then_inc(gate_in, 16)
            pool.sem_inc(w_rest.sem, 1)

            def step(n, s, half, e):
                for b in range(NB):
                    pool.wait_ge(h_main.sem, h_main.at(n, b + 1))
                    nc.gpsimd.tensor_tensor(hT[:, b % 2, 1], hidden[:], hT[:, b % 2, 0].bitcast(F32),
                                            ALU.subtract).then_inc(h_rest.sem, 1)

            order(pool, step)

        @block.scalar
        def _(act):
            act.wait_ge(gate_in, 16)
            nc.scalar.activation(tg[:, 1:2], tg[:, 0:1], ACT.Tanh).then_inc(const_ready, 1)

            def split(n, s):
                act.wait_ge(raw_in.sem, raw_in.at(n, 48))
                nc.scalar.activation(weights[:, s, 0], raw[:], ACT.Copy).then_inc(w_main.sem, 1)

            def step(n, s, half, e):
                for b in range(NB):
                    act.wait_ge(gate_sum.sem, gate_sum.at(n, b + 1))
                    nc.scalar.activation(silu[:], banks[:, 0:IC, :], ACT.Silu).then_inc(silu_done.sem, 1)
                    act.wait_ge(hidden_done.sem, hidden_done.at(n, b + 1))
                    nc.scalar.activation(hT[:, b % 2, 0], hidden[:], ACT.Copy).then_inc(h_main.sem, 1)
                    if b == 1 and not is_last(half, e):
                        split(n + 1, 1 - s)

            split(0, 0)
            order(act, step)

        @block.vector
        def _(dve):
            nc.vector.memset(unit[:], 1.0).then_inc(const_ready, 1)

            def split(n, s):
                dve.wait_ge(w_main.sem, w_main.at(n, 1))
                nc.vector.tensor_tensor(weights[:, s, 1], raw[:], weights[:, s, 0].bitcast(F32),
                                        ALU.subtract).then_inc(w_rest.sem, 1)

            def add(n, b, s):
                for t in range(TT):
                    dve.wait_ge(down_sum.sem, down_sum.at(n, b * TT + t + 1))
                    nc.vector.scalar_tensor_tensor(out=acc[:, b, t], in0=banks[:, 4 + t, :],
                                                   scalar=scale[:, s, b, t:t + 1], in1=acc[:, b, t],
                                                   op0=ALU.mult, op1=ALU.add).then_inc(added.sem, 1)

            def step(n, s, half, e):
                if e is None:
                    nc.vector.tensor_scalar(scale[:, s], unit[:], tg[:, 1:2], None, ALU.mult
                                            ).then_inc(scale_ready.sem, 1)
                else:
                    nc.vector.tensor_copy(scale[:, s], comb[:, half * NB:(half + 1) * NB, :, e]
                                          ).then_inc(scale_ready.sem, 1)
                for b in range(NB):
                    dve.wait_ge(up_sum.sem, up_sum.at(n, b + 1))
                    dve.wait_ge(silu_done.sem, silu_done.at(n, b + 1))
                    if b or not is_first(half, e):
                        dve.wait_ge(h_rest.sem, h_rest.at(n, b))
                    nc.vector.tensor_tensor(hidden[:], banks[:, IC:2 * IC, :], silu[:], ALU.mult
                                            ).then_inc(hidden_done.sem, 1)
                    if b == 0:
                        dve.wait_ge(scale_ready.sem, scale_ready.at(n, 1))
                        if not is_first(half, e):
                            if s == 0:
                                dve.wait_ge(acc_in[NB - 1], 16 * (half + 1))
                            add(n - 1, NB - 1, 1 - s)
                    else:
                        dve.wait_ge(acc_in[b - 1], 16 * (half + 1))
                        add(n, b - 1, s)
                    if b == 1 and not is_last(half, e):
                        split(n + 1, 1 - s)

            split(0, 0)
            dve.wait_ge(comb_in, 16)
            dve.wait_ge(const_ready, 2)
            order(dve, step)
            add(STEPS - 1, NB - 1, 1)

        @block.tensor
        def _(pe):
            def up(n, b, s, half, first):
                pe.wait_ge(x_in[b], 16 * (half + 1))
                if not first:
                    pe.wait_ge(hidden_done.sem, hidden_done.at(n, b))
                for is_up, done in ((False, gate_sum), (True, up_sum)):
                    for j in range(IC):
                        last = split_sum(pe, banks[:, IC * is_up + j, :],
                                         lambda a, k: gate_up(s, a, is_up, k, j), lambda a, k: xT[:, b, a, k, :],
                                         range(KC))
                    last.then_inc(done.sem, 1)

            def down_product(n, b, s, first=False):
                pe.wait_ge(h_rest.sem, h_rest.at(n, b + 1))
                for t in range(TT):
                    if not first:
                        pe.wait_ge(added.sem, added.at(n, (b - 1) * TT + t + 1))
                    split_sum(pe, banks[:, 4 + t, :], lambda a, j: hT[:, b % 2, a, j, t * P:(t + 1) * P],
                              lambda a, j: down(s, a, j), range(IC)).then_inc(down_sum.sem, 1)

            def step(n, s, half, e):
                pe.wait_ge(w_rest.sem, w_rest.at(n, 1))
                for b in range(NB):
                    up(n, b, s, half, b == 0 and is_first(half, e))
                    if b:
                        down_product(n, b - 1, s, b == 1 and is_first(half, e))
                    elif not is_first(half, e):
                        down_product(n - 1, NB - 1, 1 - s)

            order(pe, step)
            down_product(STEPS - 1, NB - 1, 1)


def program(nc, x, ctx, g_xattn, g_ffn, kv, q, proj, b_proj, w1, wq, kva, kvb, wo, w2, w_gate, e_bias,
            wg, wu, wd, swg, swu, swd, angles, out):
    def dram(name, shape):
        return nc.dram_tensor(name, shape, F32, kind="Internal").ap()

    x1 = dram("x1", (B, T, C))
    base = dram("base", (B, T, C))
    xt = dram("xt", (B, P, 2, KC, T))
    comb = dram("comb", (B, P, TT, w_gate.shape[1]))
    with nc.psum_tensor("banks", [P, 8, 512], F32) as banks:
        bank = [banks[:, n, :] for n in range(8)]
        cross_attention(nc, bank, x, ctx, kv, q, proj, b_proj, g_xattn, x1)
        self_attention_and_router(nc, bank, x1, w1, wq, kva, kvb, wo, w2, w_gate, e_bias, g_ffn, angles,
                                  base, xt, comb)
        experts(nc, banks, base, xt, comb, wg, wu, wd, swg, swu, swd, g_ffn, out)


def q_columns():
    D, J = 2 * HD, HD // 2
    plain = [(g * HG + h) * D + d for g in range(G) for d in range(HD) for h in range(HG)]
    rotated = [((2 * n + s) * HG + h) * D + HD + 2 * j + e
               for n in range(G // 2) for e in range(2) for s in range(2) for j in range(J) for h in range(HG)]
    return plain + rotated


def kva_columns(latent):
    return list(range(latent)) + [latent + 2 * j + e for e in range(2) for j in range(HD // 2)]


def rope_angles():
    import numpy as np
    f = np.float32
    freqs = (f(1.0) / f(100000.0) ** (np.arange(0, HD, 2, dtype=f) / f(HD))).astype(f)
    ang = np.outer(freqs, np.arange(T, dtype=f)).astype(f)
    t = np.repeat(np.stack([np.cos(ang), np.sin(ang)]).astype(f), HG, axis=1)
    return np.ascontiguousarray(np.concatenate([t, t], axis=1))


def kernel(**inputs):
    import numpy as np
    import concourse.bacc as bacc
    from concourse.bass_utils import run_bass_kernel_spmd as run

    a, f = "L0_xattn_", "L0_ffn_"
    a_in = {k: np.asarray(v) for k, v in inputs.items()}
    by_partition = lambda w: w.reshape(KC, P).T
    laid_out = [
        ("x", a_in["x"]), ("ctx", a_in["ctx_1024"]), ("g_xattn", a_in["g_xattn"]), ("g_ffn", a_in["g_ffn"]),
        ("W_kv", a_in[a + "W_kv"]), ("W_q", a_in[a + "W_q"]), ("W_proj", a_in[a + "W_proj"]),
        ("b_proj", a_in[a + "b_proj"]), ("w_ln1", by_partition(a_in[f + "w_ln1"])),
        ("Wq", a_in[f + "Wq"][:, q_columns()]), ("Wkva", a_in[f + "Wkva"][:, kva_columns(a_in[f + "Wkvb"].shape[0])]),
        ("Wkvb", a_in[f + "Wkvb"]), ("Wo", a_in[f + "Wo"]), ("w_ln2", by_partition(a_in[f + "w_ln2"])),
        ("Wgate", a_in[f + "Wgate"]), ("expert_bias", a_in[f + "expert_bias"]),
        ("Wg", a_in[f + "Wg"]), ("Wu", a_in[f + "Wu"]), ("Wd", a_in[f + "Wd"]),
        ("sWg", a_in[f + "sWg"]), ("sWu", a_in[f + "sWu"]), ("sWd", a_in[f + "sWd"]),
        ("angles", rope_angles()),
    ]
    nc = bacc.Bacc("TRN2", target_bir_lowering=False, num_devices=1)
    arrays, args = {}, []
    for name, array in laid_out:
        array = np.ascontiguousarray(array)
        arrays[f"in_{name}"] = array
        args.append(nc.dram_tensor(f"in_{name}", array.shape, mybir.dt.from_np(array.dtype),
                                   kind="ExternalInput").ap())
    out = nc.dram_tensor("out_0", (B, T, C), F32, kind="ExternalOutput").ap()
    program(nc, *args, out)
    r = run(nc, [arrays], core_ids=[0])
    return r.results[0]["out_0"]
```
